# Optimizing a Trainium2 kernel written in Bass

```python
import numpy as np
import jax
import jax.numpy as jnp

def _softmax(x, axis=-1):
    return jax.nn.softmax(x, axis=axis)

def _gelu(x):
    return jax.nn.gelu(x, approximate=True)

def _silu(x):
    return jax.nn.silu(x)

def _sigmoid(x):
    return jax.nn.sigmoid(x)

def _layernorm(x, axis=-1, eps=1e-05):
    m = jnp.mean(x, axis=axis, keepdims=True)
    v = jnp.var(x, axis=axis, keepdims=True)
    return (x - m) / jnp.sqrt(v + eps)

def _scatter_add(tgt, idx, src, axis=0):
    return tgt.at[idx].add(src)

def _segment_sum(src, seg, n):
    return jax.ops.segment_sum(src, seg, n)
kernel_name = 'mk_xattn_seq_d1_seqx_r2_659d9c'

def setup_inputs(seed: int=0):
    np.random.seed(seed)
    _w = jnp.asarray

    def _rec_inputs():
        import jax
        import jax.numpy as jnp
        _rk = jax.random.key(seed)
        x = -0.000296 + 1 * jax.random.normal(jax.random.fold_in(_rk, 1), (4, 2048, 640), jnp.float32)
        _lenS = 2048 - jax.random.randint(jax.random.fold_in(_rk, 7), (4,), 0, max(1, 2048 // 4) + 1, jnp.int32)
        _lenS2 = 128 - jax.random.randint(jax.random.fold_in(_rk, 8), (4,), 0, max(1, 128 // 4) + 1, jnp.int32)
        _ctx_2048P = jax.random.normal(jax.random.fold_in(_rk, 11), (4, 16, 1024), jnp.float32)
        _ctx_2048c = jax.random.dirichlet(jax.random.fold_in(_rk, 511), 0.3 * jnp.ones((16,), jnp.float32), (4, 128))
        _ctx_2048t = jnp.einsum('bsk,bkd->bsd', _ctx_2048c, _ctx_2048P)
        _ctx_2048t = _ctx_2048t * jax.lax.rsqrt(jnp.mean(jnp.square(_ctx_2048t)) + 1e-12) * 0.953939
        ctx_2048 = 0.00118529 + 0.99962 * (_ctx_2048t + 0.3 * jax.random.normal(jax.random.fold_in(_rk, 611), (4, 128, 1024), jnp.float32))
        fside_Bx4x4_0 = jax.random.uniform(jax.random.fold_in(_rk, 12), (4, 4, 4), jnp.float32, 0.0, 0.981965)
        return (x, ctx_2048, fside_Bx4x4_0)
    x, ctx_2048, fside_Bx4x4_0 = _rec_inputs()

    def _L0_xattn_setup():
        import jax, jax.numpy as jnp
        import numpy as np
        HEADS = 20
        NUM_IP_TOKENS = 4
        NUM_DUMMY_TOKENS = 4
        IP_SCALE = 1.0
        ASPECT_RATIO = 1.0
        NEG = -10000.0

        def _grid_hw(seq_len, aspect_ratio):
            width = int((seq_len / aspect_ratio) ** 0.5)
            height = seq_len // width
            while width * height != seq_len:
                if width * height < seq_len:
                    width += 1
                else:
                    width -= 1
                height = seq_len // width
            return (height, width)

        def _sdpa(q, k, v, mask=None):
            dh = q.shape[-1]
            scores = jnp.einsum('bhqd,bhkd->bhqk', q, k) / jnp.sqrt(jnp.asarray(dh, q.dtype))
            if mask is not None:
                scores = scores + mask
            probs = jax.nn.softmax(scores, axis=-1)
            return jnp.einsum('bhqk,bhkd->bhqd', probs, v)

        def _split_heads(x, heads):
            b, l, d = x.shape
            return x.reshape(b, l, heads, d // heads).transpose(0, 2, 1, 3)

        def _merge_heads(x):
            b, h, l, dh = x.shape
            return x.transpose(0, 2, 1, 3).reshape(b, l, h * dh)

        def _ip_mask(bbox, batch_size, seq_len, dtype):
            M = bbox.shape[1]
            height, width = _grid_hw(seq_len, ASPECT_RATIO)
            x = jnp.linspace(0.0, 1.0, width, dtype=dtype)
            y = jnp.linspace(0.0, 1.0, height, dtype=dtype)
            yg, xg = jnp.meshgrid(y, x, indexing='ij')
            xg = xg.reshape(-1)
            yg = yg.reshape(-1)
            x1, y1, x2, y2 = (bbox[..., 0:1], bbox[..., 1:2], bbox[..., 2:3], bbox[..., 3:4])
            inside = (xg >= x1) & (xg <= x2) & (yg >= y1) & (yg <= y2)
            ip_mask = jnp.where(inside, 0.0, NEG).astype(dtype)
            ip_mask = jnp.transpose(ip_mask, (0, 2, 1))[:, None]
            ip_mask = jnp.repeat(ip_mask, NUM_IP_TOKENS // M, axis=-1)
            dummy = jnp.where(jnp.any(inside, axis=1), NEG, 0.0).astype(dtype)
            dummy = jnp.repeat(dummy[:, None, :, None], NUM_DUMMY_TOKENS, axis=-1)
            return jnp.concatenate([dummy, ip_mask], axis=-1)
        key = jax.random.key(seed)
        ks = jax.random.split(key, 12)
        B, S, D, C = (4, 2048, 640, 1024)
        text_len, M = (77, 4)
        hidden_states = jax.random.normal(ks[0], (B, S, D), jnp.float32)
        encoder_hidden_states = jax.random.normal(ks[1], (B, text_len + NUM_IP_TOKENS + NUM_DUMMY_TOKENS, C), jnp.float32)
        p1 = jax.random.uniform(ks[2], (B, M, 2), jnp.float32)
        p2 = jax.random.uniform(ks[3], (B, M, 2), jnp.float32)
        bbox = jnp.concatenate([jnp.minimum(p1, p2), jnp.maximum(p1, p2)], axis=-1)
        s = 0.02
        w_q = jax.random.normal(ks[4], (D, D), jnp.float32) * s
        w_k = jax.random.normal(ks[5], (C, D), jnp.float32) * s
        w_v = jax.random.normal(ks[6], (C, D), jnp.float32) * s
        w_k_ip = jax.random.normal(ks[7], (C, D), jnp.float32) * s
        w_v_ip = jax.random.normal(ks[8], (C, D), jnp.float32) * s
        w_out = jax.random.normal(ks[9], (D, D), jnp.float32) * s
        b_out = jnp.zeros((D,), jnp.float32)
        return {'hidden_states': hidden_states, 'encoder_hidden_states': encoder_hidden_states, 'bbox': bbox, 'w_q': w_q, 'w_k': w_k, 'w_v': w_v, 'w_k_ip': w_k_ip, 'w_v_ip': w_v_ip, 'w_out': w_out, 'b_out': b_out}
    _L0_xattn_all = _L0_xattn_setup()
    _L0_xattn_in = {k: v for k, v in _L0_xattn_all.items() if k in ('w_q', 'w_k', 'w_v', 'w_k_ip', 'w_v_ip', 'w_out', 'b_out')}
    del _L0_xattn_all
    return {'x': x, 'ctx_2048': ctx_2048, 'fside_Bx4x4_0': fside_Bx4x4_0, 'L0_xattn_w_q': _L0_xattn_in['w_q'], 'L0_xattn_w_k': _L0_xattn_in['w_k'], 'L0_xattn_w_v': _L0_xattn_in['w_v'], 'L0_xattn_w_k_ip': _L0_xattn_in['w_k_ip'], 'L0_xattn_w_v_ip': _L0_xattn_in['w_v_ip'], 'L0_xattn_w_out': _L0_xattn_in['w_out'], 'L0_xattn_b_out': _L0_xattn_in['b_out']}

def reference(x, ctx_2048, fside_Bx4x4_0, L0_xattn_w_q, L0_xattn_w_k, L0_xattn_w_v, L0_xattn_w_k_ip, L0_xattn_w_v_ip, L0_xattn_w_out, L0_xattn_b_out):
    import jax
    import jax.numpy as jnp

    def _L0_xattn_ref(hidden_states, encoder_hidden_states, bbox, w_q, w_k, w_v, w_k_ip, w_v_ip, w_out, b_out):
        import jax, jax.numpy as jnp
        import numpy as np
        HEADS = 20
        NUM_IP_TOKENS = 4
        NUM_DUMMY_TOKENS = 4
        IP_SCALE = 1.0
        ASPECT_RATIO = 1.0
        NEG = -10000.0

        def _grid_hw(seq_len, aspect_ratio):
            width = int((seq_len / aspect_ratio) ** 0.5)
            height = seq_len // width
            while width * height != seq_len:
                if width * height < seq_len:
                    width += 1
                else:
                    width -= 1
                height = seq_len // width
            return (height, width)

        def _sdpa(q, k, v, mask=None):
            dh = q.shape[-1]
            scores = jnp.einsum('bhqd,bhkd->bhqk', q, k) / jnp.sqrt(jnp.asarray(dh, q.dtype))
            if mask is not None:
                scores = scores + mask
            probs = jax.nn.softmax(scores, axis=-1)
            return jnp.einsum('bhqk,bhkd->bhqd', probs, v)

        def _split_heads(x, heads):
            b, l, d = x.shape
            return x.reshape(b, l, heads, d // heads).transpose(0, 2, 1, 3)

        def _merge_heads(x):
            b, h, l, dh = x.shape
            return x.transpose(0, 2, 1, 3).reshape(b, l, h * dh)

        def _ip_mask(bbox, batch_size, seq_len, dtype):
            M = bbox.shape[1]
            height, width = _grid_hw(seq_len, ASPECT_RATIO)
            x = jnp.linspace(0.0, 1.0, width, dtype=dtype)
            y = jnp.linspace(0.0, 1.0, height, dtype=dtype)
            yg, xg = jnp.meshgrid(y, x, indexing='ij')
            xg = xg.reshape(-1)
            yg = yg.reshape(-1)
            x1, y1, x2, y2 = (bbox[..., 0:1], bbox[..., 1:2], bbox[..., 2:3], bbox[..., 3:4])
            inside = (xg >= x1) & (xg <= x2) & (yg >= y1) & (yg <= y2)
            ip_mask = jnp.where(inside, 0.0, NEG).astype(dtype)
            ip_mask = jnp.transpose(ip_mask, (0, 2, 1))[:, None]
            ip_mask = jnp.repeat(ip_mask, NUM_IP_TOKENS // M, axis=-1)
            dummy = jnp.where(jnp.any(inside, axis=1), NEG, 0.0).astype(dtype)
            dummy = jnp.repeat(dummy[:, None, :, None], NUM_DUMMY_TOKENS, axis=-1)
            return jnp.concatenate([dummy, ip_mask], axis=-1)
        B, S, D = hidden_states.shape
        residual = hidden_states
        end_pos = encoder_hidden_states.shape[1] - (NUM_IP_TOKENS + NUM_DUMMY_TOKENS)
        text = encoder_hidden_states[:, :end_pos]
        ip_h = encoder_hidden_states[:, end_pos:]
        q = _split_heads(hidden_states @ w_q, HEADS)
        k = _split_heads(text @ w_k, HEADS)
        v = _split_heads(text @ w_v, HEADS)
        out_text = _sdpa(q, k, v)
        out_text = _merge_heads(out_text)
        mask_ip = _ip_mask(bbox, B, S, hidden_states.dtype)
        k_ip = _split_heads(ip_h @ w_k_ip, HEADS)
        v_ip = _split_heads(ip_h @ w_v_ip, HEADS)
        out_ip = _merge_heads(_sdpa(q, k_ip, v_ip, mask=mask_ip))
        out = out_text + IP_SCALE * out_ip
        out = out @ w_out + b_out
        out = out + residual
        return out
    x = _L0_xattn_ref(x, ctx_2048, fside_Bx4x4_0, L0_xattn_w_q, L0_xattn_w_k, L0_xattn_w_v, L0_xattn_w_k_ip, L0_xattn_w_v_ip, L0_xattn_w_out, L0_xattn_b_out)
    return x

_drawn_inputs = setup_inputs


def setup_inputs(seed=0):
    import zlib

    import numpy as np

    out = dict(_drawn_inputs(seed))
    spreads = {'L0_xattn_b_out': (0.0, 0.1)}
    factors = {'L0_xattn_w_k': 2.964}
    for name, (base, spread) in spreads.items():
        noise = np.random.default_rng([zlib.crc32(name.encode()), seed]).standard_normal(out[name].shape)
        drawn = base * np.exp(spread * noise) if base else spread * noise
        out[name] = jnp.asarray(drawn.astype(out[name].dtype))
    for name, factor in factors.items():
        out[name] = (out[name] * factor).astype(out[name].dtype)
    return out
```

```python
from contextlib import ExitStack

import numpy as np

import concourse.bass as bass
from concourse import mybir

F32 = mybir.dt.float32
F32R = mybir.dt.float32r
ALU = mybir.AluOpType
ACT = mybir.ActivationFunctionType
AX_X = mybir.AxisListType.X

P = 128
B, S, D, C = 4, 2048, 640, 1024
HEADS, DH = 20, 32
KEYS, TEXT, IP = 128, 120, 8
BOXES = 4
W = 512
J = P // DH
G = HEADS // J
RT = W // P
TILES = B * S // W
TPB = S // W
CK = C // P
NEG = -10000.0
SCALE = float(DH) ** -0.5
STACK = 3 * DH + 1
IPROWS = 3 * J * IP
GRID_W, GRID_H = 64, 32
assert GRID_W * GRID_H == S


def wait(engine, sem, value):
    if isinstance(value, int) and value <= 0:
        return
    engine.wait_ge(sem, value)


def snap(engine, value):
    return value if isinstance(value, int) else engine.snap(value)


def xattn_kernel(nc, xT, ctxT, boxes, gx, gy, ident, wq, wk, wv, wkip, wvip, wo, bo, outT):
    def scratch(name, shape, dt):
        return nc.dram_tensor(name, shape, dt, kind="Internal").ap()

    kt_hi_d = scratch("kt_hi_d", (P, G, B * KEYS), F32)
    kt_lo_d = scratch("kt_lo_d", (P, G, B * KEYS), F32)
    v_d = scratch("v_d", (B, TEXT, D), F32)
    vip_hi_d = scratch("vip_hi_d", (B, IP, D), F32)
    vip_lo_d = scratch("vip_lo_d", (B, IP, D), F32)

    with ExitStack() as ctx:
        def sb(name, shape, dt=F32, where=None):
            return (where or ctx).enter_context(nc.sbuf_tensor(name, shape, dt))

        def sem(name):
            return ctx.enter_context(nc.semaphore(name))

        wq_hi = sb("wq_hi", [P, G, D], F32R)
        wq_lo = sb("wq_lo", [P, G, D], F32R)
        wo_hi = sb("wo_hi", [P, G, D], F32R)
        wo_lo = sb("wo_lo", [P, G, D], F32R)
        bias = sb("bias", [P, G])
        idn = sb("idn", [P, P])
        mask = sb("mask", [P, TILES * RT, IP])
        keys_done = sem("keys_done")

        keys_and_values(nc, ctx, sb, sem, ctxT, boxes, gx, gy, ident, wq, wk, wv, wkip, wvip, wo, bo,
                        wq_hi, wq_lo, wo_hi, wo_lo, bias, idn, mask,
                        kt_hi_d, kt_lo_d, v_d, vip_hi_d, vip_lo_d)
        attention(nc, ctx, sb, sem, xT, outT, wq_hi, wq_lo, wo_hi, wo_lo, bias, idn, mask,
                  kt_hi_d, kt_lo_d, v_d, vip_hi_d, vip_lo_d)


def keys_and_values(nc, ctx, sb, sem, ctxT, boxes, gx, gy, ident, wq, wk, wv, wkip, wvip, wo, bo,
                    wq_hi, wq_lo, wo_hi, wo_lo, bias, idn, mask,
                    kt_hi_d, kt_lo_d, v_d, vip_hi_d, vip_lo_d):
    HALF = D // 2
    ALL_TEXT = B * TEXT
    with ExitStack() as temp:
        ctx_sb = sb("ctx_sb", [P, CK, B * KEYS], F32, temp)
        w_a = sb("w_a", [P, CK, D], F32, temp)
        w_b = sb("w_b", [P, CK, D], F32, temp)
        w_c = sb("w_c", [P, CK, D], F32, temp)
        w_raw = sb("w_raw", [P, G, D], F32, temp)
        kt_hi = sb("kt_hi", [P, G, B * KEYS], F32R, temp)
        kt_lo = sb("kt_lo", [P, G, B * KEYS], F32R, temp)
        v_sb = sb("v_sb", [TEXT, B, D], F32, temp)
        vip_hi = sb("vip_hi", [B * IP, D], F32R, temp)
        vip_lo = sb("vip_lo", [B * IP, D], F32R, temp)
        box = sb("box", [P, B, BOXES * 4], F32, temp)
        grid_x = sb("grid_x", [P, 1], F32, temp)
        grid_y = sb("grid_y", [P, B * BOXES, S // P], F32, temp)
        inside = sb("inside", [P, B, S // P, BOXES], F32, temp)
        test_x = sb("test_x", [P, B, BOXES, 2], F32, temp)
        test_y = sb("test_y", [P, 2, S // P], F32, temp)
        anybox = sb("anybox", [P, B, S // P], F32, temp)
        bank = [temp.enter_context(nc.psum_tensor(f"kv_bank{i}", [P, W], F32)) for i in range(4)]

        raw_loaded = [sem("wq_loaded"), sem("wo_loaded")]
        small_loaded = sem("small_loaded")
        ctx_loaded = sem("ctx_loaded")
        w_loaded = {n: sem(f"{n}_loaded") for n in ("wk", "wkip", "wv", "wvip")}
        group_mm = sem("kv_group_mm")
        group_read = sem("kv_group_read")
        group_lo = sem("kv_group_lo")
        raw_hi = sem("raw_hi")
        raw_lo = sem("raw_lo")
        mask_step = sem("mask_step")
        stored = sem("kv_stored")

        K_BANKS, V_BANKS, IP_BANKS = G, 2 * B, 2
        FILLS = K_BANKS + V_BANKS + IP_BANKS

        with nc.Block() as block:
            @block.sync
            def _(sp):
                sp.dma_start(ctx_sb[:, :, :], ctxT.rearrange("(k p) n -> p k n", p=P)).then_inc(ctx_loaded, 16)
                sp.dma_start(w_a[:, :, :], wk.rearrange("(k p) n -> p k n", p=P)).then_inc(w_loaded["wk"], 16)
                sp.dma_start(w_b[:, :, :], wkip.rearrange("(k p) n -> p k n", p=P)).then_inc(w_loaded["wkip"], 16)
                sp.dma_start(w_raw[:, :, :], wq.rearrange("(k p) n -> p k n", p=P)).then_inc(raw_loaded[0], 16)
                sp.dma_start(w_c[:, :, :], wv.rearrange("(k p) n -> p k n", p=P)).then_inc(w_loaded["wv"], 16)
                sp.dma_start(idn[:, :], ident).then_inc(small_loaded, 16)
                sp.dma_start(bias[:, :], bo.rearrange("(p g) -> p g", g=G)).then_inc(small_loaded, 16)
                sp.dma_start(grid_x[:, :], gx).then_inc(small_loaded, 16)
                sp.dma_start(grid_y[:, :, :], gy).then_inc(small_loaded, 16)
                sp.dma_start(box[:, :, :].rearrange("p b n -> p (b n)"),
                             boxes.to_broadcast([P, B * BOXES * 4])).then_inc(small_loaded, 16)
                sp.wait_ge(group_mm, K_BANKS)
                sp.dma_start(w_a[:, :, :], wvip.rearrange("(k p) n -> p k n", p=P)).then_inc(w_loaded["wvip"], 16)
                sp.wait_ge(raw_hi, 1)
                sp.wait_ge(raw_lo, 1)
                sp.dma_start(w_raw[:, :, :], wo.rearrange("(k p) n -> p k n", p=P)).then_inc(raw_loaded[1], 16)
                sp.wait_ge(group_read, K_BANKS)
                sp.dma_start(kt_hi_d, kt_hi[:, :, :].bitcast(F32)).then_inc(stored, 16)
                sp.wait_ge(group_lo, K_BANKS)
                sp.dma_start(kt_lo_d, kt_lo[:, :, :].bitcast(F32)).then_inc(stored, 16)
                sp.wait_ge(group_read, K_BANKS + V_BANKS)
                sp.dma_start(v_d.rearrange("b p n -> p b n"), v_sb[:, :, :]).then_inc(stored, 16)
                sp.wait_ge(group_read, FILLS)
                sp.dma_start(vip_hi_d.rearrange("b k n -> (b k) n"), vip_hi[:, :].bitcast(F32)).then_inc(stored, 16)
                sp.wait_ge(group_lo, K_BANKS + IP_BANKS)
                sp.dma_start(vip_lo_d.rearrange("b k n -> (b k) n"), vip_lo[:, :].bitcast(F32)).then_inc(stored, 16)
                sp.wait_ge(stored, 5 * 16)

            @block.tensor
            def _(pe):
                pe.wait_ge(ctx_loaded, 16)
                pe.wait_ge(w_loaded["wk"], 16)
                pe.wait_ge(w_loaded["wkip"], 16)
                for g in range(G):
                    if g >= 4:
                        pe.wait_ge(group_read, g - 3)
                        pe.wait_ge(group_lo, g - 3)
                    for k in range(CK):
                        nc.tensor.matmul(bank[g % 4][:, 0:ALL_TEXT], w_a[:, k, g * P:(g + 1) * P],
                                         ctx_sb[:, k, 0:ALL_TEXT], start=k == 0, stop=k == CK - 1)
                    for k in range(CK):
                        last = nc.tensor.matmul(bank[g % 4][:, ALL_TEXT:], w_b[:, k, g * P:(g + 1) * P],
                                                ctx_sb[:, k, ALL_TEXT:], start=k == 0, stop=k == CK - 1)
                    last.then_inc(group_mm, 1)
                pe.wait_ge(w_loaded["wv"], 16)
                for n in range(K_BANKS, FILLS):
                    pe.wait_ge(group_read, n - 3)
                    if n - 4 < K_BANKS:
                        pe.wait_ge(group_lo, n - 3)
                    half = (n - K_BANKS) % 2
                    if n < K_BANKS + V_BANKS:
                        b = (n - K_BANKS) // 2
                        for k in range(CK):
                            last = nc.tensor.matmul(bank[n % 4][0:TEXT, 0:HALF], ctx_sb[:, k, b * TEXT:(b + 1) * TEXT],
                                                    w_c[:, k, half * HALF:(half + 1) * HALF],
                                                    start=k == 0, stop=k == CK - 1)
                    else:
                        pe.wait_ge(w_loaded["wvip"], 16)
                        for k in range(CK):
                            last = nc.tensor.matmul(bank[n % 4][0:B * IP, 0:HALF], ctx_sb[:, k, ALL_TEXT:],
                                                    w_a[:, k, half * HALF:(half + 1) * HALF],
                                                    start=k == 0, stop=k == CK - 1)
                    last.then_inc(group_mm, 1)

            @block.scalar
            def _(act):
                def split_raw(i, hi):
                    act.wait_ge(raw_loaded[i], 16)
                    nc.scalar.activation(hi[:, :, :], w_raw[:, :, :], ACT.Copy).then_inc(raw_hi, 1)

                for g in range(G):
                    act.wait_ge(group_mm, g + 1)
                    nc.scalar.activation(kt_hi[:, g, :], bank[g % 4][:, :], ACT.Copy).then_inc(group_read, 1)
                split_raw(0, wq_hi)
                for n in range(K_BANKS, FILLS):
                    act.wait_ge(group_mm, n + 1)
                    half = (n - K_BANKS) % 2
                    part = slice(half * HALF, (half + 1) * HALF)
                    if n < K_BANKS + V_BANKS:
                        nc.scalar.activation(v_sb[:, (n - K_BANKS) // 2, part], bank[n % 4][0:TEXT, 0:HALF],
                                             ACT.Copy).then_inc(group_read, 1)
                    else:
                        nc.scalar.activation(vip_hi[:, part], bank[n % 4][0:B * IP, 0:HALF],
                                             ACT.Copy).then_inc(group_read, 1)
                    if n == K_BANKS + 1:
                        split_raw(1, wo_hi)

            @block.vector
            def _(dve):
                steps = 0

                def step(instruction):
                    nonlocal steps
                    steps += 1
                    instruction.then_inc(mask_step, 1)
                    dve.wait_ge(mask_step, steps)

                dve.wait_ge(small_loaded, 5 * 16)
                bv = box[:, :, :].rearrange("p b (m c) -> p b m c", m=BOXES)
                nc.vector.tensor_scalar(test_x[:, :, :, 0], bv[:, :, :, 0], grid_x[:, 0:1], None, ALU.is_le)
                step(nc.vector.tensor_scalar(test_x[:, :, :, 1], bv[:, :, :, 2], grid_x[:, 0:1], None, ALU.is_ge))
                step(nc.vector.tensor_tensor(test_x[:, :, :, 0], test_x[:, :, :, 0], test_x[:, :, :, 1], ALU.mult))
                for b in range(B):
                    for m in range(BOXES):
                        nc.vector.tensor_scalar(test_y[:, 0, :], grid_y[:, 0, :], bv[:, b, m, 1:2],
                                                test_x[:, b, m, 0:1], ALU.is_ge, ALU.mult)
                        step(nc.vector.tensor_scalar(test_y[:, 1, :], grid_y[:, 0, :], bv[:, b, m, 3:4],
                                                     None, ALU.is_le))
                        step(nc.vector.tensor_tensor(inside[:, b, :, m], test_y[:, 0, :], test_y[:, 1, :],
                                                     ALU.mult))
                step(nc.vector.tensor_reduce(anybox[:, :, :], inside[:, :, :, :], AX_X, ALU.max))
                rows = mask[:, :, :].rearrange("p (b r) k -> p b r k", b=B)
                for m in range(BOXES):
                    nc.vector.tensor_scalar(rows[:, :, :, m], anybox[:, :, :], NEG, None, ALU.mult)
                step(nc.vector.tensor_scalar(rows[:, :, :, BOXES:IP], inside[:, :, :, :], -NEG, NEG,
                                             ALU.mult, ALU.add))
                for g in range(G):
                    dve.wait_ge(group_read, g + 1)
                    nc.vector.tensor_tensor(kt_lo[:, g, :], bank[g % 4][:, :], kt_hi[:, g, :].bitcast(F32),
                                            ALU.subtract).then_inc(group_lo, 1)
                for i, (hi, lo) in enumerate(((wq_hi, wq_lo), (wo_hi, wo_lo))):
                    dve.wait_ge(raw_loaded[i], 16)
                    dve.wait_ge(raw_hi, i + 1)
                    nc.vector.tensor_tensor(lo[:, :, :], w_raw[:, :, :], hi[:, :, :].bitcast(F32),
                                            ALU.subtract).then_inc(raw_lo, 1)
                for half in range(2):
                    n = K_BANKS + V_BANKS + half
                    dve.wait_ge(group_read, n + 1)
                    part = slice(half * HALF, (half + 1) * HALF)
                    nc.vector.tensor_tensor(vip_lo[:, part], bank[n % 4][0:B * IP, 0:HALF],
                                            vip_hi[:, part].bitcast(F32), ALU.subtract).then_inc(group_lo, 1)


def attention(nc, ctx, sb, sem, xT, outT, wq_hi, wq_lo, wo_hi, wo_lo, bias, idn, mask,
              kt_hi_d, kt_lo_d, v_d, vip_hi_d, vip_lo_d):
    x_sb = sb("x_sb", [P, 2 * G * W])
    x_hi = sb("x_hi", [P, G, W], F32R)
    x_lo = sb("x_lo", [P, G, W], F32R)
    q_hi = sb("q_hi", [P, 2, W], F32R)
    q_lo = sb("q_lo", [P, 2, W], F32R)
    stack = sb("stack", [P, G, J, W], F32R)
    probs = sb("probs", [TEXT, J, W])
    att = sb("att", [P, W])
    att_hi = sb("att_hi", [P, G, W], F32R)
    att_lo = sb("att_lo", [P, G, W], F32R)
    sums = sb("sums", [P, W])
    rsum = sb("rsum", [P, RT, J])
    maxes = sb("maxes", [P, RT, J])
    neg_max = sb("neg_max", [J, W], F32R)
    ip_s = sb("ip_s", [P, RT * J, IP])
    ip_x = sb("ip_x", [P, RT * J, IP])
    ip_e = sb("ip_e", [P, RT * J, IP])
    ip_n = sb("ip_n", [P, RT, J * IP])
    ip_max = sb("ip_max", [P, RT * J])
    ip_sum = sb("ip_sum", [P, RT * J])
    ip_rec = sb("ip_rec", [P, RT * J])
    ip_p = sb("ip_p", [P, RT, 3, J * IP])
    ip_t = sb("ip_t", [IPROWS, W], F32R)
    ones = sb("ones", [TEXT, DH])
    kb = sb("kb", [P, G, J * KEYS], F32R)
    kb_lo = sb("kb_lo", [P, G, J * IP], F32R)
    kst = sb("kst", [STACK, J, G, TEXT], F32R)
    v_sb = sb("v_now", [TEXT, D])
    vst = sb("vst", [IPROWS, G, P], F32R)

    def psum(name):
        return ctx.enter_context(nc.psum_tensor(name, [P, W], F32))

    q_bank = psum("q_bank")
    a_bank = [psum(f"a_bank{i}") for i in range(2)]
    s_bank = ctx.enter_context(nc.psum_tensor("s_bank", [P, 2, W], F32))
    pv_bank = psum("pv_bank")
    l_bank = psum("l_bank")
    t_bank = psum("t_bank")

    x_loaded = [sem(f"x_loaded{k}") for k in range(G)]
    out_stored = [sem(f"out_stored{k}") for k in range(G)]
    q_stacked = [sem(f"q_stacked{g}") for g in range(G)]
    m_stacked = [sem(f"m_stacked{g}") for g in range(G)]
    kb_loaded = sem("kb_loaded")
    kst_loaded = sem("kst_loaded")
    v_loaded = sem("v_loaded")
    vst_loaded = sem("vst_loaded")
    q_mm, bound_mm, score_mm, pv_mm = sem("q_mm"), sem("bound_mm"), sem("score_mm"), sem("pv_mm")
    sums_turned, rsum_turned, ipv_mm = sem("sums_turned"), sem("rsum_turned"), sem("ipv_mm")
    ip_turned, max_turned, out_mm = sem("ip_turned"), sem("max_turned"), sem("out_mm")
    q_hi_done, exp_done, sums_copied = sem("q_hi_done"), sem("exp_done"), sem("sums_copied")
    rsum_copied, ip_copied, max_copied = sem("rsum_copied"), sem("ip_copied"), sem("max_copied")
    ip_exp_done, att_hi_done, x_hi_done = sem("ip_exp_done"), sem("att_hi_done"), sem("x_hi_done")
    q_lo_done, bound_read, rsum_done = sem("q_lo_done"), sem("bound_read"), sem("rsum_done")
    rsum_step = sem("rsum_step")
    scaled_done, att_done, out_done = sem("scaled_done"), sem("att_done"), sem("out_done")
    ip_max_done, ip_sub_done = sem("ip_max_done"), sem("ip_sub_done")
    ip_sum_done, ip_rec_done = sem("ip_sum_done"), sem("ip_rec_done")
    cleared, ip_norm_done = sem("cleared"), sem("ip_norm_done")
    ip_p_done, att_lo_done, x_lo_done = sem("ip_p_done"), sem("att_lo_done"), sem("x_lo_done")

    UNITS = TILES * G
    CLEARED = 5
    KB_DMAS, KST_DMAS, V_DMAS, VST_DMAS = 3 * J, 3, 1, 3 * J

    def earlier(t, g, lag):
        return (t, g - lag) if g >= lag else (t - 1, g - lag + G)

    def no_more(count):
        return min(count, UNITS) if isinstance(count, int) else count

    def x_slot(t, k):
        return (t % 2) * (G * W) + k * W

    def runs(t, g):
        return not isinstance(t, int) or 0 <= t < TILES

    def batches(t):
        return t // TPB + 1

    def over_tiles(engine, iteration):
        iteration(0)
        with engine.Fori(1, TILES) as t:
            iteration(t)
        iteration(TILES)

    with nc.Block() as block:

        @block.sync
        def _(sp):
            def load_x(t):
                column = snap(sp, t * W)
                for k in range(G):
                    slot = snap(sp, x_slot(t, k))
                    wait(sp, out_stored[k], 16 * (t - 1))
                    sp.dma_start(x_sb[:, bass.ds(slot, W)],
                                 xT[k * P:(k + 1) * P, bass.ds(column, W)]).then_inc(x_loaded[k], 16)

            def load_kb(b):
                wait(sp, bound_mm, RT * G * TPB * b)
                for j in range(J):
                    rows = slice(j, P, J)
                    sp.dma_start(kb[rows, :, j * TEXT:(j + 1) * TEXT].bitcast(F32),
                                 kt_hi_d[rows, :, bass.ds(b * TEXT, TEXT)]).then_inc(kb_loaded, 16)
                    at = J * TEXT + j * IP
                    sp.dma_start(kb[rows, :, at:at + IP].bitcast(F32),
                                 kt_hi_d[rows, :, bass.ds(B * TEXT + b * IP, IP)]).then_inc(kb_loaded, 16)
                    sp.dma_start(kb_lo[rows, :, j * IP:(j + 1) * IP].bitcast(F32),
                                 kt_lo_d[rows, :, bass.ds(B * TEXT + b * IP, IP)]).then_inc(kb_loaded, 16)

            def load_kst_v(b):
                wait(sp, score_mm, 2 * G * TPB * b)
                for i, src in enumerate((kt_hi_d, kt_hi_d, kt_lo_d)):
                    sp.dma_start(kst[i * DH:(i + 1) * DH, :, :, :].bitcast(F32).rearrange("r j g n -> r (j g) n"),
                                 src[:, :, bass.ds(b * TEXT, TEXT)]).then_inc(kst_loaded, 16)
                wait(sp, pv_mm, G * TPB * b)
                sp.dma_start(v_sb[:, :], v_d[b, :, :]).then_inc(v_loaded, 16)

            def load_vst(b):
                wait(sp, ipv_mm, G * TPB * b)
                for i, src in enumerate((vip_hi_d, vip_hi_d, vip_lo_d)):
                    for j in range(J):
                        at = (i * J + j) * IP
                        sp.dma_start(vst[at:at + IP, :, j * DH:(j + 1) * DH].bitcast(F32),
                                     src[b, :, :].rearrange("k (g n) -> k g n", g=G)[:, :, j * DH:(j + 1) * DH]
                                     ).then_inc(vst_loaded, 16)

            def iteration(t, batch=None):
                front = runs(t, 0)
                for g in range(G):
                    if g == 0 and batch is not None:
                        load_kb(batch)
                    if g == 3 and batch is not None:
                        load_kst_v(batch)
                    if front:
                        for i, (src, made) in enumerate(((q_hi, q_hi_done), (q_lo, q_lo_done), (q_hi, q_hi_done))):
                            if i < 2:
                                sp.wait_ge(made, G * t + g + 1)
                            sp.dma_start(stack[i * DH:(i + 1) * DH, g, :, :].bitcast(F32), src[:, g % 2, :].bitcast(F32)
                                         ).then_inc(q_stacked[g], 16)
                    if g == 3 and batch is not None:
                        load_vst(batch)
                    ta, ga = earlier(t, g, 1)
                    if runs(ta, ga):
                        sp.wait_ge(max_copied, G * ta + ga + 1)
                        sp.dma_start(stack[3 * DH:STACK, ga, :, :].bitcast(F32), neg_max[:, :].bitcast(F32)).then_inc(m_stacked[ga], 16)
                    if g == 3 and runs(t - 1, 0):
                        column = snap(sp, (t - 1) * W)
                        for m in range(G):
                            slot = snap(sp, x_slot(t - 1, m))
                            sp.wait_ge(out_done, G * (t - 1) + m + 1)
                            sp.dma_start(outT[m * P:(m + 1) * P, bass.ds(column, W)],
                                         x_sb[:, bass.ds(slot, W)]).then_inc(out_stored[m], 16)
                    if g == 3 and front and not (isinstance(t, int) and t == TILES - 1):
                        load_x(t + 1)

            load_x(0)
            sp.wait_ge(cleared, CLEARED)
            load_kb(0)
            load_kst_v(0)
            load_vst(0)
            iteration(0)
            with sp.Fori(0, B - 1) as b:
                for i in range(1, TPB + 1):
                    iteration(b * TPB + i, batch=b + 1 if i == TPB else None)
            for t in range((B - 1) * TPB + 1, TILES + 1):
                iteration(t)
            for k in range(G):
                sp.wait_ge(out_stored[k], 16 * TILES)

        @block.tensor
        def _(pe):
            def project(t, g, k):
                if g == 0:
                    pe.wait_ge(x_hi_done, G * t + k + 1)
                    pe.wait_ge(x_lo_done, G * t + k + 1)
                if k == 0:
                    wait(pe, q_lo_done, G * t + g)
                    if g == 4:
                        wait(pe, out_done, G * (t - 1) + 4)
                cols = slice(g * P, (g + 1) * P)
                nc.tensor.matmul(q_bank[:, :], wq_hi[:, k, cols], x_lo[:, k, :], start=k == 0, stop=False)
                nc.tensor.matmul(q_bank[:, :], wq_lo[:, k, cols], x_hi[:, k, :], start=False, stop=False)
                last = nc.tensor.matmul(q_bank[:, :], wq_hi[:, k, cols], x_hi[:, k, :],
                                        start=False, stop=k == G - 1)
                if k == G - 1:
                    last.then_inc(q_mm, 1)

            def bound(t, g, rt):
                if rt == 0:
                    pe.wait_ge(q_hi_done, G * t + g + 1)
                    pe.wait_ge(q_lo_done, G * t + g + 1)
                    if g == 0:
                        pe.wait_ge(kb_loaded, 16 * KB_DMAS * batches(t))
                wait(pe, bound_read, RT * (G * t + g) + rt - 1)
                bank, rows = a_bank[rt % 2], slice(rt * P, (rt + 1) * P)
                ip = slice(J * TEXT, J * KEYS)
                nc.tensor.matmul(bank[:, :], q_hi[:, g % 2, rows], kb[:, g, :], start=True, stop=False)
                nc.tensor.matmul(bank[:, ip], q_hi[:, g % 2, rows], kb_lo[:, g, :], start=False, stop=False)
                nc.tensor.matmul(bank[:, ip], q_lo[:, g % 2, rows], kb[:, g, ip],
                                 start=False, stop=True).then_inc(bound_mm, 1)

            def score(t, g, pair):
                if pair == 0:
                    pe.wait_ge(q_stacked[g], 3 * 16 * (t + 1))
                    pe.wait_ge(m_stacked[g], 16 * (t + 1))
                    if g == 0:
                        pe.wait_ge(kst_loaded, 16 * KST_DMAS * batches(t))
                wait(pe, exp_done, 2 * (G * t + g) + pair)
                for i in range(2):
                    j = 2 * pair + i
                    last = nc.tensor.matmul(s_bank[0:TEXT, i, :], kst[:, j, g, :], stack[0:STACK, g, j, :],
                                            start=True, stop=True)
                last.then_inc(score_mm, 1)

            def values(t, g):
                u = G * t + g
                if g == 0:
                    pe.wait_ge(v_loaded, 16 * V_DMAS * batches(t))
                pe.wait_ge(exp_done, 2 * u + 2)
                wait(pe, scaled_done, u)
                wait(pe, att_done, u)
                for j in range(J):
                    h = J * g + j
                    nc.tensor.matmul(pv_bank[j * DH:(j + 1) * DH, :], v_sb[:, h * DH:(h + 1) * DH],
                                     probs[:, j, :], start=True, stop=True)
                for j in range(J):
                    last = nc.tensor.matmul(l_bank[j * DH:(j + 1) * DH, :], ones[:, :], probs[:, j, :],
                                            start=True, stop=True)
                last.then_inc(pv_mm, 1)

            def turn_sums(t, g):
                pe.wait_ge(sums_copied, G * t + g + 1)
                for rt in range(RT):
                    last = nc.tensor.transpose(l_bank[:, rt * P:(rt + 1) * P], sums[:, rt * P:(rt + 1) * P],
                                               idn[:, :])
                last.then_inc(sums_turned, 1)

            def turn_rsums(t, g):
                pe.wait_ge(rsum_done, G * t + g + 1)
                for rt in range(RT):
                    last = nc.tensor.transpose(l_bank[:, rt * P:(rt + 1) * P], sums[:, rt * P:(rt + 1) * P],
                                               idn[:, :])
                last.then_inc(rsum_turned, 1)

            def ip_values(t, g):
                pe.wait_ge(rsum_copied, G * t + g + 1)
                pe.wait_ge(ip_copied, G * t + g + 1)
                if g == 0:
                    pe.wait_ge(vst_loaded, 16 * VST_DMAS * batches(t))
                nc.tensor.matmul(l_bank[:, :], vst[:, g, :], ip_t[:, :], start=True, stop=True
                                 ).then_inc(ipv_mm, 1)

            def turn_ip(t, g):
                u = G * t + g
                pe.wait_ge(ip_p_done, u + 1)
                wait(pe, max_copied, no_more(u + 2))
                for rt in range(RT):
                    last = nc.tensor.transpose(t_bank[0:IPROWS, rt * P:(rt + 1) * P],
                                               ip_p[:, rt, :, :].rearrange("p a n -> p (a n)"), idn[:, :])
                last.then_inc(ip_turned, 1)

            def turn_max(t, g, slot_t, slot):
                u = G * t + g
                pe.wait_ge(bound_read, RT * (u + 1))
                wait(pe, ip_copied, u - 1)
                if slot == 3:
                    wait(pe, out_done, G * slot_t)
                for rt in range(RT):
                    last = nc.tensor.transpose(t_bank[0:J, rt * P:(rt + 1) * P], maxes[:, rt, :], idn[:, :])
                last.then_inc(max_turned, 1)

            def output(t):
                for m in range(G):
                    bank = q_bank if m % 2 else t_bank
                    if m == 0:
                        pe.wait_ge(ip_copied, no_more(G * (t + 1) + 1))
                    elif m == 1:
                        wait(pe, q_lo_done, no_more(G * (t + 1) + 4))
                    else:
                        pe.wait_ge(out_done, G * t + m - 1)
                    cols = slice(m * P, (m + 1) * P)
                    for k in range(G):
                        if m == 0:
                            pe.wait_ge(att_hi_done, G * t + k + 1)
                            pe.wait_ge(att_lo_done, G * t + k + 1)
                        nc.tensor.matmul(bank[:, :], wo_hi[:, k, cols], att_lo[:, k, :], start=k == 0, stop=False)
                        nc.tensor.matmul(bank[:, :], wo_lo[:, k, cols], att_hi[:, k, :], start=False, stop=False)
                        last = nc.tensor.matmul(bank[:, :], wo_hi[:, k, cols], att_hi[:, k, :],
                                                start=False, stop=k == G - 1)
                    last.then_inc(out_mm, 1)

            def iteration(t):
                for g in range(G):
                    now, a, s, c = (t, g), earlier(t, g, 1), earlier(t, g, 3), earlier(t, g, 4)
                    if runs(*s):
                        score(*s, 0)
                    if runs(*now):
                        project(*now, 0)
                    if runs(*c):
                        turn_sums(*c)
                    if runs(*now):
                        project(*now, 1)
                    if runs(*a):
                        bound(*a, 0)
                        bound(*a, 1)
                    if runs(*c):
                        turn_rsums(*c)
                    if runs(*s):
                        score(*s, 1)
                    if runs(*now):
                        project(*now, 2)
                        project(*now, 3)
                    if runs(*c):
                        ip_values(*c)
                    if runs(*s):
                        turn_ip(*s)
                    if runs(*a):
                        bound(*a, 2)
                    if runs(*now):
                        project(*now, 4)
                    if runs(*a):
                        bound(*a, 3)
                    if g == 3 and runs(t - 1, 0):
                        output(t - 1)
                    if runs(*s):
                        values(*s)
                    if runs(*a):
                        turn_max(*a, t, g)

            over_tiles(pe, iteration)

        @block.scalar
        def _(act):
            def exps(t, g, pair):
                u = G * t + g
                act.wait_ge(score_mm, 2 * u + pair + 1)
                wait(act, pv_mm, u)
                nc.scalar.activation(probs[:, 2 * pair:2 * pair + 2, :], s_bank[0:TEXT, :, :], ACT.Exp,
                                     scale=SCALE).then_inc(exp_done, 1)

            def copy_rsums(t, g):
                u = G * t + g
                act.wait_ge(rsum_turned, u + 1)
                wait(act, att_lo_done, u)
                nc.scalar.activation(att[:, :], l_bank[:, :], ACT.Copy).then_inc(rsum_copied, 1)

            def copy_ip(t, g):
                u = G * t + g
                act.wait_ge(ip_turned, u + 1)
                wait(act, ipv_mm, u)
                nc.scalar.activation(ip_t[:, :], t_bank[0:IPROWS, :], ACT.Copy).then_inc(ip_copied, 1)

            def att_high(t, g):
                act.wait_ge(att_done, G * t + g + 1)
                wait(act, out_mm, G * t)
                nc.scalar.activation(att_hi[:, g, :], att[:, :], ACT.Copy).then_inc(att_hi_done, 1)

            def q_high(t, g):
                u = G * t + g
                act.wait_ge(q_mm, u + 1)
                lag = 1 if g == 0 else 2
                wait(act, bound_mm, RT * (u - lag + 1))
                tp, gp = earlier(t, g, lag)
                if runs(tp, gp):
                    act.wait_ge(q_stacked[gp], 3 * 16 * (tp + 1))
                nc.scalar.activation(q_hi[:, g % 2, :], q_bank[:, :], ACT.Copy).then_inc(q_hi_done, 1)

            def copy_sums(t, g):
                u = G * t + g
                act.wait_ge(pv_mm, u + 1)
                wait(act, rsum_turned, u)
                nc.scalar.activation(sums[:, :], l_bank[:, :], ACT.Copy).then_inc(sums_copied, 1)

            def copy_max(t, g):
                act.wait_ge(max_turned, G * t + g + 1)
                tp, gp = earlier(t, g, 1)
                if runs(tp, gp):
                    act.wait_ge(m_stacked[gp], 16 * (tp + 1))
                nc.scalar.activation(neg_max[:, :], t_bank[0:J, :], ACT.Copy, scale=-1.0).then_inc(max_copied, 1)

            def ip_exps(t, g):
                u = G * t + g
                act.wait_ge(ip_sub_done, u + 1)
                wait(act, ip_norm_done, u)
                nc.scalar.activation(ip_e[:, :, :], ip_x[:, :, :], ACT.Exp).then_inc(ip_exp_done, 1)

            def x_high(t):
                for k in range(G):
                    slot = snap(act, x_slot(t, k))
                    act.wait_ge(x_loaded[k], 16 * (t + 1))
                    wait(act, q_mm, G * t)
                    nc.scalar.activation(x_hi[:, k, :], x_sb[:, bass.ds(slot, W)], ACT.Copy
                                         ).then_inc(x_hi_done, 1)

            def iteration(t):
                for g in range(G):
                    now, a, s, c = (t, g), earlier(t, g, 1), earlier(t, g, 3), earlier(t, g, 4)
                    if runs(*s):
                        exps(*s, 0)
                    if runs(*c):
                        copy_rsums(*c)
                    if runs(*s):
                        exps(*s, 1)
                        copy_ip(*s)
                    if runs(*c):
                        att_high(*c)
                    if runs(*now):
                        q_high(*now)
                    if g == 4 and runs(*now) and not (isinstance(t, int) and t == TILES - 1):
                        pass
                    if runs(*s):
                        copy_sums(*s)
                    if runs(*a):
                        copy_max(*a)
                        ip_exps(*a)

            def tiles():
                x_high(0)
                iteration(0)
                x_high(1)
                with act.Fori(1, TILES - 1) as t:
                    iteration(t)
                    x_high(t + 1)
                iteration(TILES - 1)
                iteration(TILES)

            tiles()

        @block.vector
        def _(dve):
            def read_bound(t, g, rt):
                u = G * t + g
                bank = a_bank[rt % 2]
                dve.wait_ge(bound_mm, RT * u + rt + 1)
                if rt == 0:
                    wait(dve, max_turned, u)
                    wait(dve, ip_sub_done, u)
                nc.vector.tensor_reduce(maxes[:, rt, :],
                                        bank[:, 0:J * TEXT].rearrange("p (j n) -> p j n", j=J), AX_X, ALU.max)
                row = mask[:, bass.ds(t * RT + rt, 1), :].to_broadcast([P, J, IP])
                nc.vector.scalar_tensor_tensor(
                    ip_s[:, rt * J:(rt + 1) * J, :],
                    bank[:, J * TEXT:J * KEYS].rearrange("p (j n) -> p j n", j=J),
                    SCALE, row, ALU.mult, ALU.add).then_inc(bound_read, 1)

            def reciprocal(t, g):
                u = G * t + g
                dve.wait_ge(sums_turned, u + 1)
                nc.vector.reciprocal(rsum[:, :, :],
                                     l_bank[:, :].rearrange("p (r j d) -> p r j d", r=RT, j=J)[:, :, :, 0]
                                     ).then_inc(rsum_step, 1)
                dve.wait_ge(rsum_step, u + 1)
                nc.vector.tensor_copy(sums[:, :].rearrange("p (r j d) -> p r j d", r=RT, j=J),
                                      rsum[:, :, :].unsqueeze(3).to_broadcast([P, RT, J, DH])
                                      ).then_inc(rsum_done, 1)

            def ip_sums(t, g):
                u = G * t + g
                dve.wait_ge(ip_exp_done, u + 1)
                wait(dve, ip_rec_done, u)
                nc.vector.tensor_reduce(ip_sum[:, :], ip_e[:, :, :], AX_X, ALU.add).then_inc(ip_sum_done, 1)
                wait(dve, ip_norm_done, u)
                dve.wait_ge(ip_sum_done, u + 1)
                nc.vector.reciprocal(ip_rec[:, :], ip_sum[:, :]).then_inc(ip_rec_done, 1)

            def scale_values(t, g):
                u = G * t + g
                dve.wait_ge(rsum_copied, u + 1)
                dve.wait_ge(pv_mm, u + 1)
                nc.vector.tensor_tensor(att[:, :], pv_bank[:, :], att[:, :], ALU.mult).then_inc(scaled_done, 1)

            def add_ip(t, g):
                u = G * t + g
                dve.wait_ge(ipv_mm, u + 1)
                dve.wait_ge(scaled_done, u + 1)
                nc.vector.tensor_tensor(att[:, :], l_bank[:, :], att[:, :], ALU.add).then_inc(att_done, 1)

            def ip_shift(t, g):
                u = G * t + g
                dve.wait_ge(bound_read, RT * (u + 1))
                nc.vector.tensor_reduce(ip_max[:, :], ip_s[:, :, :], AX_X, ALU.max).then_inc(ip_max_done, 1)
                wait(dve, ip_exp_done, u)
                dve.wait_ge(ip_max_done, u + 1)
                nc.vector.tensor_tensor(ip_x[:, :, :], ip_s[:, :, :],
                                        ip_max[:, :].unsqueeze(2).to_broadcast([P, RT * J, IP]),
                                        ALU.subtract).then_inc(ip_sub_done, 1)

            def q_low(t, g):
                u = G * t + g
                dve.wait_ge(q_hi_done, u + 1)
                nc.vector.tensor_tensor(q_lo[:, g % 2, :], q_bank[:, :], q_hi[:, g % 2, :].bitcast(F32),
                                        ALU.subtract).then_inc(q_lo_done, 1)

            def finish(t):
                for m in range(G):
                    place = x_sb[:, bass.ds(snap(dve, x_slot(t, m)), W)]
                    dve.wait_ge(out_mm, G * t + m + 1)
                    bank = q_bank if m % 2 else t_bank
                    nc.vector.scalar_tensor_tensor(place, bank[:, :], bias[:, m:m + 1], place,
                                                   ALU.add, ALU.add).then_inc(out_done, 1)

            def iteration(t):
                for g in range(G):
                    now, a, i, c = (t, g), earlier(t, g, 1), earlier(t, g, 2), earlier(t, g, 4)
                    if runs(*c):
                        reciprocal(*c)
                    if runs(*a):
                        read_bound(*a, 0)
                        read_bound(*a, 1)
                    if runs(*i):
                        ip_sums(*i)
                    if runs(*c):
                        scale_values(*c)
                        add_ip(*c)
                    if runs(*a):
                        read_bound(*a, 2)
                        read_bound(*a, 3)
                        ip_shift(*a)
                    if runs(*now):
                        q_low(*now)
                    if g == 3 and runs(t - 1, 0):
                        finish(t - 1)

            nc.vector.memset(ones[:, :], 1.0).then_inc(cleared, 1)
            nc.vector.memset(kst[3 * DH:STACK, :, :, :].bitcast(F32), 1.0).then_inc(cleared, 1)
            over_tiles(dve, iteration)

        @block.gpsimd
        def _(pool):
            def ip_parts(t, g):
                u = G * t + g
                pool.wait_ge(ip_rec_done, u + 1)
                wait(pool, ip_p_done, u)
                wait(pool, ip_turned, u)
                e = ip_e[:, :, :].rearrange("p (r j) n -> p r j n", r=RT)
                rec = ip_rec[:, :].rearrange("p (r j) -> p r j", r=RT).unsqueeze(3).to_broadcast([P, RT, J, IP])
                for out in (ip_n[:, :, :], ip_p[:, :, 0, :].bitcast(F32R), ip_p[:, :, 2, :].bitcast(F32R)):
                    last = nc.gpsimd.tensor_tensor(out.rearrange("p r (j n) -> p r j n", j=J), e, rec, ALU.mult)
                last.then_inc(ip_norm_done, 1)
                pool.wait_ge(ip_norm_done, u + 1)
                nc.gpsimd.tensor_tensor(ip_p[:, :, 1, :].bitcast(F32R), ip_n[:, :, :], ip_p[:, :, 0, :],
                                        ALU.subtract).then_inc(ip_p_done, 1)

            def att_low(t, g):
                pool.wait_ge(att_hi_done, G * t + g + 1)
                nc.gpsimd.tensor_tensor(att_lo[:, g, :], att[:, :], att_hi[:, g, :].bitcast(F32),
                                        ALU.subtract).then_inc(att_lo_done, 1)

            def x_low(t):
                for k in range(G):
                    place = x_sb[:, bass.ds(snap(pool, x_slot(t, k)), W)]
                    pool.wait_ge(x_hi_done, G * t + k + 1)
                    nc.gpsimd.tensor_tensor(x_lo[:, k, :], place, x_hi[:, k, :].bitcast(F32),
                                            ALU.subtract).then_inc(x_lo_done, 1)

            def iteration(t):
                for g in range(G):
                    i, c = earlier(t, g, 2), earlier(t, g, 4)
                    if runs(*i):
                        ip_parts(*i)
                    if runs(*c):
                        att_low(*c)

            nc.gpsimd.memset(kb[:, :, :].bitcast(F32), 0.0).then_inc(cleared, 1)
            nc.gpsimd.memset(kb_lo[:, :, :].bitcast(F32), 0.0).then_inc(cleared, 1)
            nc.gpsimd.memset(vst[:, :, :].bitcast(F32), 0.0).then_inc(cleared, 1)
            x_low(0)
            iteration(0)
            x_low(1)
            with pool.Fori(1, TILES - 1) as t:
                iteration(t)
                x_low(t + 1)
            iteration(TILES - 1)
            iteration(TILES)


def kernel(**inputs):
    import concourse.bacc as bacc
    from concourse.bass_utils import run_bass_kernel_spmd

    def a(name):
        return np.asarray(inputs[name])

    def by_feature(w):
        return np.ascontiguousarray(w.reshape(w.shape[0], G, J, DH).transpose(0, 1, 3, 2).reshape(w.shape[0], D))

    xs = np.linspace(0.0, 1.0, GRID_W, dtype=np.float32)
    ys = np.linspace(0.0, 1.0, GRID_H, dtype=np.float32)
    token = np.arange(S).reshape(S // P, P)
    gx = xs[token[0] % GRID_W].reshape(P, 1)
    gy = np.repeat(ys[token // GRID_W].T[:, None, :], B * BOXES, axis=1)

    c = a("ctx_2048")
    arrays = {
        "xT": np.ascontiguousarray(a("x").reshape(B * S, D).T),
        "ctxT": np.ascontiguousarray(np.concatenate([c[:, :TEXT].reshape(B * TEXT, C), c[:, TEXT:].reshape(B * IP, C)]).T),
        "boxes": a("fside_Bx4x4_0").reshape(1, B * BOXES * 4),
        "gx": gx, "gy": np.ascontiguousarray(gy),
        "ident": np.eye(P, dtype=np.float32),
        "wq": by_feature(a("L0_xattn_w_q")),
        "wk": by_feature(a("L0_xattn_w_k")),
        "wv": a("L0_xattn_w_v"),
        "wkip": by_feature(a("L0_xattn_w_k_ip")),
        "wvip": a("L0_xattn_w_v_ip"),
        "wo": a("L0_xattn_w_out"),
        "bo": np.ascontiguousarray(a("L0_xattn_b_out").reshape(G, P).T.reshape(D)),
    }
    nc = bacc.Bacc("TRN2", target_bir_lowering=False, num_devices=1)
    args = [nc.dram_tensor(n, v.shape, mybir.dt.from_np(v.dtype), kind="ExternalInput").ap()
            for n, v in arrays.items()]
    args.append(nc.dram_tensor("outT", (D, B * S), F32, kind="ExternalOutput").ap())
    xattn_kernel(nc, *args)
    r = run_bass_kernel_spmd(nc, [arrays], core_ids=[0])
    return np.ascontiguousarray(r.results[0]["outT"].T).reshape(B, S, D)
```

```python
from contextlib import ExitStack

import numpy as np

import concourse.bass as bass
from concourse import mybir

F32 = mybir.dt.float32
F32R = mybir.dt.float32r
ALU = mybir.AluOpType
ACT = mybir.ActivationFunctionType
AX_X = mybir.AxisListType.X

P = 128
B, S, D, C = 4, 2048, 640, 1024
HEADS, DH = 20, 32
KEYS, TEXT, IP = 128, 120, 8
BOXES = 4
W = 512
J = P // DH
G = HEADS // J
RT = W // P
TILES = B * S // W
TPB = S // W
CK = C // P
NEG = -10000.0
SCALE = float(DH) ** -0.5
STACK = 3 * DH + 1
IPROWS = 3 * J * IP
TURNED = IPROWS + J
GRID_W, GRID_H = 64, 32
assert GRID_W * GRID_H == S


def wait(engine, sem, value):
    if isinstance(value, int) and value <= 0:
        return
    engine.wait_ge(sem, value)


def snap(engine, value):
    return value if isinstance(value, int) else engine.snap(value)


def xattn_kernel(nc, xT, ctxT, boxes, gx, gy, ident, wq, wk, wv, wkip, wvip, wo, bo, outT):
    def scratch(name, shape, dt):
        return nc.dram_tensor(name, shape, dt, kind="Internal").ap()

    kt_hi_d = scratch("kt_hi_d", (P, G, B * KEYS), F32)
    kt_lo_d = scratch("kt_lo_d", (P, G, B * KEYS), F32)
    v_d = scratch("v_d", (B, TEXT, D), F32)
    vip_hi_d = scratch("vip_hi_d", (B, IP, D), F32)
    vip_lo_d = scratch("vip_lo_d", (B, IP, D), F32)

    with ExitStack() as ctx:
        def sb(name, shape, dt=F32, where=None):
            return (where or ctx).enter_context(nc.sbuf_tensor(name, shape, dt))

        def sem(name):
            return ctx.enter_context(nc.semaphore(name))

        wq_hi = sb("wq_hi", [P, G, D], F32R)
        wq_lo = sb("wq_lo", [P, G, D], F32R)
        wo_hi = sb("wo_hi", [P, G, D], F32R)
        wo_lo = sb("wo_lo", [P, G, D], F32R)
        bias = sb("bias", [P, G])
        idn = sb("idn", [P, P])
        mask = sb("mask", [P, TILES * RT, IP])
        keys_done = sem("keys_done")

        keys_and_values(nc, ctx, sb, sem, ctxT, boxes, gx, gy, ident, wq, wk, wv, wkip, wvip, wo, bo,
                        wq_hi, wq_lo, wo_hi, wo_lo, bias, idn, mask,
                        kt_hi_d, kt_lo_d, v_d, vip_hi_d, vip_lo_d)
        attention(nc, ctx, sb, sem, xT, outT, wq_hi, wq_lo, wo_hi, wo_lo, bias, idn, mask,
                  kt_hi_d, kt_lo_d, v_d, vip_hi_d, vip_lo_d)


def keys_and_values(nc, ctx, sb, sem, ctxT, boxes, gx, gy, ident, wq, wk, wv, wkip, wvip, wo, bo,
                    wq_hi, wq_lo, wo_hi, wo_lo, bias, idn, mask,
                    kt_hi_d, kt_lo_d, v_d, vip_hi_d, vip_lo_d):
    HALF = D // 2
    ALL_TEXT = B * TEXT
    with ExitStack() as temp:
        ctx_sb = sb("ctx_sb", [P, CK, B * KEYS], F32, temp)
        w_a = sb("w_a", [P, CK, D], F32, temp)
        w_b = sb("w_b", [P, CK, D], F32, temp)
        w_c = sb("w_c", [P, CK, D], F32, temp)
        w_raw = sb("w_raw", [P, G, D], F32, temp)
        kt_hi = sb("kt_hi", [P, G, B * KEYS], F32R, temp)
        kt_lo = sb("kt_lo", [P, G, B * KEYS], F32R, temp)
        v_sb = sb("v_sb", [TEXT, B, D], F32, temp)
        vip_hi = sb("vip_hi", [B * IP, D], F32R, temp)
        vip_lo = sb("vip_lo", [B * IP, D], F32R, temp)
        box = sb("box", [P, B, BOXES * 4], F32, temp)
        grid_x = sb("grid_x", [P, 1], F32, temp)
        grid_y = sb("grid_y", [P, B * BOXES, S // P], F32, temp)
        inside = sb("inside", [P, B, S // P, BOXES], F32, temp)
        test_x = sb("test_x", [P, B, BOXES, 2], F32, temp)
        test_y = sb("test_y", [P, 2, S // P], F32, temp)
        anybox = sb("anybox", [P, B, S // P], F32, temp)
        bank = [temp.enter_context(nc.psum_tensor(f"kv_bank{i}", [P, W], F32)) for i in range(4)]

        raw_loaded = [sem("wq_loaded"), sem("wo_loaded")]
        small_loaded = sem("small_loaded")
        ctx_loaded = sem("ctx_loaded")
        w_loaded = {n: sem(f"{n}_loaded") for n in ("wk", "wkip", "wv", "wvip")}
        group_mm = sem("kv_group_mm")
        group_read = sem("kv_group_read")
        group_lo = sem("kv_group_lo")
        raw_hi = sem("raw_hi")
        raw_lo = sem("raw_lo")
        mask_step = sem("mask_step")
        stored = sem("kv_stored")

        K_BANKS, V_BANKS, IP_BANKS = G, 2 * B, 2
        FILLS = K_BANKS + V_BANKS + IP_BANKS

        with nc.Block() as block:
            @block.sync
            def _(sp):
                sp.dma_start(ctx_sb[:, :, :], ctxT.rearrange("(k p) n -> p k n", p=P)).then_inc(ctx_loaded, 16)
                sp.dma_start(w_a[:, :, :], wk.rearrange("(k p) n -> p k n", p=P)).then_inc(w_loaded["wk"], 16)
                sp.dma_start(w_b[:, :, :], wkip.rearrange("(k p) n -> p k n", p=P)).then_inc(w_loaded["wkip"], 16)
                sp.dma_start(w_raw[:, :, :], wq.rearrange("(k p) n -> p k n", p=P)).then_inc(raw_loaded[0], 16)
                sp.dma_start(w_c[:, :, :], wv.rearrange("(k p) n -> p k n", p=P)).then_inc(w_loaded["wv"], 16)
                sp.dma_start(idn[:, :], ident).then_inc(small_loaded, 16)
                sp.dma_start(bias[:, :], bo.rearrange("(p g) -> p g", g=G)).then_inc(small_loaded, 16)
                sp.dma_start(grid_x[:, :], gx).then_inc(small_loaded, 16)
                sp.dma_start(grid_y[:, :, :], gy).then_inc(small_loaded, 16)
                sp.dma_start(box[:, :, :].rearrange("p b n -> p (b n)"),
                             boxes.to_broadcast([P, B * BOXES * 4])).then_inc(small_loaded, 16)
                sp.wait_ge(group_mm, K_BANKS)
                sp.dma_start(w_a[:, :, :], wvip.rearrange("(k p) n -> p k n", p=P)).then_inc(w_loaded["wvip"], 16)
                sp.wait_ge(raw_hi, 1)
                sp.wait_ge(raw_lo, 1)
                sp.dma_start(w_raw[:, :, :], wo.rearrange("(k p) n -> p k n", p=P)).then_inc(raw_loaded[1], 16)
                sp.wait_ge(group_read, K_BANKS)
                sp.dma_start(kt_hi_d, kt_hi[:, :, :].bitcast(F32)).then_inc(stored, 16)
                sp.wait_ge(group_lo, K_BANKS)
                sp.dma_start(kt_lo_d, kt_lo[:, :, :].bitcast(F32)).then_inc(stored, 16)
                sp.wait_ge(group_read, K_BANKS + V_BANKS)
                sp.dma_start(v_d.rearrange("b p n -> p b n"), v_sb[:, :, :]).then_inc(stored, 16)
                sp.wait_ge(group_read, FILLS)
                sp.dma_start(vip_hi_d.rearrange("b k n -> (b k) n"), vip_hi[:, :].bitcast(F32)).then_inc(stored, 16)
                sp.wait_ge(group_lo, K_BANKS + IP_BANKS)
                sp.dma_start(vip_lo_d.rearrange("b k n -> (b k) n"), vip_lo[:, :].bitcast(F32)).then_inc(stored, 16)
                sp.wait_ge(stored, 5 * 16)

            @block.tensor
            def _(pe):
                pe.wait_ge(ctx_loaded, 16)
                pe.wait_ge(w_loaded["wk"], 16)
                pe.wait_ge(w_loaded["wkip"], 16)
                for g in range(G):
                    if g >= 4:
                        pe.wait_ge(group_read, g - 3)
                        pe.wait_ge(group_lo, g - 3)
                    for k in range(CK):
                        nc.tensor.matmul(bank[g % 4][:, 0:ALL_TEXT], w_a[:, k, g * P:(g + 1) * P],
                                         ctx_sb[:, k, 0:ALL_TEXT], start=k == 0, stop=k == CK - 1)
                    for k in range(CK):
                        last = nc.tensor.matmul(bank[g % 4][:, ALL_TEXT:], w_b[:, k, g * P:(g + 1) * P],
                                                ctx_sb[:, k, ALL_TEXT:], start=k == 0, stop=k == CK - 1)
                    last.then_inc(group_mm, 1)
                pe.wait_ge(w_loaded["wv"], 16)
                for n in range(K_BANKS, FILLS):
                    pe.wait_ge(group_read, n - 3)
                    if n - 4 < K_BANKS:
                        pe.wait_ge(group_lo, n - 3)
                    half = (n - K_BANKS) % 2
                    if n < K_BANKS + V_BANKS:
                        b = (n - K_BANKS) // 2
                        for k in range(CK):
                            last = nc.tensor.matmul(bank[n % 4][0:TEXT, 0:HALF], ctx_sb[:, k, b * TEXT:(b + 1) * TEXT],
                                                    w_c[:, k, half * HALF:(half + 1) * HALF],
                                                    start=k == 0, stop=k == CK - 1)
                    else:
                        pe.wait_ge(w_loaded["wvip"], 16)
                        for k in range(CK):
                            last = nc.tensor.matmul(bank[n % 4][0:B * IP, 0:HALF], ctx_sb[:, k, ALL_TEXT:],
                                                    w_a[:, k, half * HALF:(half + 1) * HALF],
                                                    start=k == 0, stop=k == CK - 1)
                    last.then_inc(group_mm, 1)

            @block.scalar
            def _(act):
                def split_raw(i, hi):
                    act.wait_ge(raw_loaded[i], 16)
                    nc.scalar.activation(hi[:, :, :], w_raw[:, :, :], ACT.Copy).then_inc(raw_hi, 1)

                for g in range(G):
                    act.wait_ge(group_mm, g + 1)
                    nc.scalar.activation(kt_hi[:, g, :], bank[g % 4][:, :], ACT.Copy).then_inc(group_read, 1)
                split_raw(0, wq_hi)
                for n in range(K_BANKS, FILLS):
                    act.wait_ge(group_mm, n + 1)
                    half = (n - K_BANKS) % 2
                    part = slice(half * HALF, (half + 1) * HALF)
                    if n < K_BANKS + V_BANKS:
                        nc.scalar.activation(v_sb[:, (n - K_BANKS) // 2, part], bank[n % 4][0:TEXT, 0:HALF],
                                             ACT.Copy).then_inc(group_read, 1)
                    else:
                        nc.scalar.activation(vip_hi[:, part], bank[n % 4][0:B * IP, 0:HALF],
                                             ACT.Copy).then_inc(group_read, 1)
                    if n == K_BANKS + 1:
                        split_raw(1, wo_hi)

            @block.vector
            def _(dve):
                steps = 0

                def step(instruction):
                    nonlocal steps
                    steps += 1
                    instruction.then_inc(mask_step, 1)
                    dve.wait_ge(mask_step, steps)

                dve.wait_ge(small_loaded, 5 * 16)
                bv = box[:, :, :].rearrange("p b (m c) -> p b m c", m=BOXES)
                nc.vector.tensor_scalar(test_x[:, :, :, 0], bv[:, :, :, 0], grid_x[:, 0:1], None, ALU.is_le)
                step(nc.vector.tensor_scalar(test_x[:, :, :, 1], bv[:, :, :, 2], grid_x[:, 0:1], None, ALU.is_ge))
                step(nc.vector.tensor_tensor(test_x[:, :, :, 0], test_x[:, :, :, 0], test_x[:, :, :, 1], ALU.mult))
                for b in range(B):
                    for m in range(BOXES):
                        nc.vector.tensor_scalar(test_y[:, 0, :], grid_y[:, 0, :], bv[:, b, m, 1:2],
                                                test_x[:, b, m, 0:1], ALU.is_ge, ALU.mult)
                        step(nc.vector.tensor_scalar(test_y[:, 1, :], grid_y[:, 0, :], bv[:, b, m, 3:4],
                                                     None, ALU.is_le))
                        step(nc.vector.tensor_tensor(inside[:, b, :, m], test_y[:, 0, :], test_y[:, 1, :],
                                                     ALU.mult))
                step(nc.vector.tensor_reduce(anybox[:, :, :], inside[:, :, :, :], AX_X, ALU.max))
                rows = mask[:, :, :].rearrange("p (b r) k -> p b r k", b=B)
                for m in range(BOXES):
                    nc.vector.tensor_scalar(rows[:, :, :, m], anybox[:, :, :], NEG, None, ALU.mult)
                step(nc.vector.tensor_scalar(rows[:, :, :, BOXES:IP], inside[:, :, :, :], -NEG, NEG,
                                             ALU.mult, ALU.add))
                for g in range(G):
                    dve.wait_ge(group_read, g + 1)
                    nc.vector.tensor_tensor(kt_lo[:, g, :], bank[g % 4][:, :], kt_hi[:, g, :].bitcast(F32),
                                            ALU.subtract).then_inc(group_lo, 1)
                for i, (hi, lo) in enumerate(((wq_hi, wq_lo), (wo_hi, wo_lo))):
                    dve.wait_ge(raw_loaded[i], 16)
                    dve.wait_ge(raw_hi, i + 1)
                    nc.vector.tensor_tensor(lo[:, :, :], w_raw[:, :, :], hi[:, :, :].bitcast(F32),
                                            ALU.subtract).then_inc(raw_lo, 1)
                for half in range(2):
                    n = K_BANKS + V_BANKS + half
                    dve.wait_ge(group_read, n + 1)
                    part = slice(half * HALF, (half + 1) * HALF)
                    nc.vector.tensor_tensor(vip_lo[:, part], bank[n % 4][0:B * IP, 0:HALF],
                                            vip_hi[:, part].bitcast(F32), ALU.subtract).then_inc(group_lo, 1)


def attention(nc, ctx, sb, sem, xT, outT, wq_hi, wq_lo, wo_hi, wo_lo, bias, idn, mask,
              kt_hi_d, kt_lo_d, v_d, vip_hi_d, vip_lo_d):
    x_sb = sb("x_sb", [P, 2 * G * W])
    out_sb = sb("out_sb", [P, 2, W])
    x_hi = sb("x_hi", [P, G, W], F32R)
    x_lo = sb("x_lo", [P, G, W], F32R)
    q_hi = sb("q_hi", [P, 2, W], F32R)
    q_lo = sb("q_lo", [P, 2, W], F32R)
    stack = sb("stack", [P, G, J, W], F32R)
    probs = sb("probs", [TEXT, J, W])
    att = sb("att", [P, W])
    att_hi = sb("att_hi", [P, G, W], F32R)
    att_lo = sb("att_lo", [P, G, W], F32R)
    rough = sb("rough", [P, W])
    ip_s = sb("ip_s", [P, RT * J, IP])
    ip_x = sb("ip_x", [P, RT * J, IP])
    ip_e = sb("ip_e", [P, RT * J, IP])
    ip_n = sb("ip_n", [P, RT, J * IP])
    ip_max = sb("ip_max", [P, RT * J])
    ip_sum = sb("ip_sum", [P, RT * J])
    ip_rec = sb("ip_rec", [P, RT * J])
    by_query = sb("by_query", [P, RT, TURNED])
    by_row = sb("by_row", [TURNED, W], F32R)
    one = sb("one", [P, 1])
    ones = sb("ones", [TEXT, DH])
    kb = sb("kb", [P, G, J * KEYS], F32R)
    kb_lo = sb("kb_lo", [P, G, J * IP], F32R)
    kst = sb("kst", [STACK, J, G, TEXT], F32R)
    v_sb = sb("v_now", [TEXT, D])
    vst = sb("vst", [IPROWS, G, P], F32R)

    def psum(name):
        return ctx.enter_context(nc.psum_tensor(name, [P, W], F32))

    q_bank = psum("q_bank")
    a_bank = [psum(f"a_bank{i}") for i in range(2)]
    s_bank = ctx.enter_context(nc.psum_tensor("s_bank", [P, 2, W], F32))
    pv_bank = psum("pv_bank")
    l_bank = psum("l_bank")
    t_bank = psum("t_bank")

    x_loaded = [sem(f"x_loaded{k}") for k in range(G)]
    out_stored = [sem(f"out_stored{i}") for i in range(2)]
    q_stacked = [sem(f"q_stacked{g}") for g in range(G)]
    m_stacked = [sem(f"m_stacked{g}") for g in range(G)]
    kb_loaded = sem("kb_loaded")
    kst_loaded = sem("kst_loaded")
    v_loaded = sem("v_loaded")
    vst_loaded = sem("vst_loaded")
    q_mm, bound_mm, score_mm, pv_mm = sem("q_mm"), sem("bound_mm"), sem("score_mm"), sem("pv_mm")
    ipv_mm, turned, out_mm, x_used = sem("ipv_mm"), sem("turned"), sem("out_mm"), sem("x_used")
    q_hi_done, exp_done, rows_copied = sem("q_hi_done"), sem("exp_done"), sem("rows_copied")
    ln_done, rough_done = sem("ln_done"), sem("rough_done")
    ip_exp_done, att_hi_done, x_hi_done = sem("ip_exp_done"), sem("att_hi_done"), sem("x_hi_done")
    q_lo_done, bound_read = sem("q_lo_done"), sem("bound_read")
    sums_read, refined = sem("sums_read"), sem("refined")
    scaled_done, att_done, out_done = sem("scaled_done"), sem("att_done"), sem("out_done")
    ip_max_done, ip_sub_done = sem("ip_max_done"), sem("ip_sub_done")
    ip_sum_done, ip_rec_done = sem("ip_sum_done"), sem("ip_rec_done")
    cleared, ip_norm_done, ip_hi_done = sem("cleared"), sem("ip_norm_done"), sem("ip_hi_done")
    ip_p_done, att_lo_done, x_lo_done = sem("ip_p_done"), sem("att_lo_done"), sem("x_lo_done")

    UNITS = TILES * G
    CLEARED = 7
    KB_DMAS, KST_DMAS, V_DMAS, VST_DMAS = 3 * J, 3, 1, 3 * J

    def earlier(t, g, lag):
        return (t, g - lag) if g >= lag else (t - 1, g - lag + G)

    def no_more(count):
        return min(count, UNITS) if isinstance(count, int) else count

    def stores_before(t, m):
        return t * len(range(m % 2, G, 2)) + m // 2

    def x_slot(t, k):
        return (t % 2) * (G * W) + k * W

    def runs(t, g):
        return not isinstance(t, int) or 0 <= t < TILES

    def has_next(t):
        return not isinstance(t, int) or t < TILES - 1

    def batches(t):
        return t // TPB + 1

    def over_tiles(engine, iteration):
        iteration(0)
        with engine.Fori(1, TILES) as t:
            iteration(t)
        iteration(TILES)

    with nc.Block() as block:

        @block.sync
        def _(sp):
            def load_x(t, k):
                column = snap(sp, t * W)
                slot = snap(sp, x_slot(t, k))
                wait(sp, out_done, G * (t - 2) + k + 1)
                sp.dma_start(x_sb[:, bass.ds(slot, W)],
                             xT[k * P:(k + 1) * P, bass.ds(column, W)]).then_inc(x_loaded[k], 16)

            def store(t, m):
                column = snap(sp, t * W)
                sp.wait_ge(out_done, G * t + m + 1)
                sp.dma_start(outT[m * P:(m + 1) * P, bass.ds(column, W)],
                             out_sb[:, m % 2, :]).then_inc(out_stored[m % 2], 16)

            def load_kb(b):
                wait(sp, bound_mm, RT * G * TPB * b)
                for j in range(J):
                    rows = slice(j, P, J)
                    sp.dma_start(kb[rows, :, j * TEXT:(j + 1) * TEXT].bitcast(F32),
                                 kt_hi_d[rows, :, bass.ds(b * TEXT, TEXT)]).then_inc(kb_loaded, 16)
                    at = J * TEXT + j * IP
                    sp.dma_start(kb[rows, :, at:at + IP].bitcast(F32),
                                 kt_hi_d[rows, :, bass.ds(B * TEXT + b * IP, IP)]).then_inc(kb_loaded, 16)
                    sp.dma_start(kb_lo[rows, :, j * IP:(j + 1) * IP].bitcast(F32),
                                 kt_lo_d[rows, :, bass.ds(B * TEXT + b * IP, IP)]).then_inc(kb_loaded, 16)

            def load_kst(b):
                wait(sp, score_mm, 2 * G * TPB * b)
                for i, src in enumerate((kt_hi_d, kt_hi_d, kt_lo_d)):
                    sp.dma_start(kst[i * DH:(i + 1) * DH, :, :, :].bitcast(F32).rearrange("r j g n -> r (j g) n"),
                                 src[:, :, bass.ds(b * TEXT, TEXT)]).then_inc(kst_loaded, 16)

            def load_v(b):
                wait(sp, pv_mm, G * TPB * b)
                sp.dma_start(v_sb[:, :], v_d[b, :, :]).then_inc(v_loaded, 16)

            def load_vst(b):
                wait(sp, ipv_mm, G * TPB * b)
                for i, src in enumerate((vip_hi_d, vip_hi_d, vip_lo_d)):
                    for j in range(J):
                        at = (i * J + j) * IP
                        sp.dma_start(vst[at:at + IP, :, j * DH:(j + 1) * DH].bitcast(F32),
                                     src[b, :, :].rearrange("k (g n) -> k g n", g=G)[:, :, j * DH:(j + 1) * DH]
                                     ).then_inc(vst_loaded, 16)

            def iteration(t, batch=None):
                front = runs(t, 0)
                for g in range(G):
                    if g == 0 and batch is not None:
                        load_kb(batch)
                    if g == 2 and batch is not None:
                        load_kst(batch)
                    if g == 3 and batch is not None:
                        load_v(batch)
                    if front:
                        for i, (src, made) in enumerate(((q_hi, q_hi_done), (q_lo, q_lo_done), (q_hi, q_hi_done))):
                            if i < 2:
                                sp.wait_ge(made, G * t + g + 1)
                            sp.dma_start(stack[i * DH:(i + 1) * DH, g, :, :].bitcast(F32), src[:, g % 2, :].bitcast(F32)
                                         ).then_inc(q_stacked[g], 16)
                    if g == 3 and batch is not None:
                        load_vst(batch)
                    if g == 3:
                        for m in range(G):
                            if runs(t - 1, 0):
                                store(t - 1, m)
                            if front and has_next(t):
                                load_x(t + 1, m)
                    ta, ga = earlier(t, g, 1)
                    if runs(ta, ga):
                        sp.wait_ge(rows_copied, G * t + g)
                        sp.dma_start(stack[3 * DH:STACK, ga, :, :].bitcast(F32),
                                     by_row[IPROWS:TURNED, :].bitcast(F32)).then_inc(m_stacked[ga], 16)
            for k in range(G):
                load_x(0, k)
            sp.wait_ge(cleared, CLEARED)
            load_kb(0)
            load_kst(0)
            load_v(0)
            load_vst(0)
            iteration(0)
            with sp.Fori(0, B - 1) as b:
                for i in range(1, TPB + 1):
                    iteration(b * TPB + i, batch=b + 1 if i == TPB else None)
            for t in range((B - 1) * TPB + 1, TILES + 1):
                iteration(t)
            for i in range(2):
                sp.wait_ge(out_stored[i], 16 * stores_before(TILES, i))

        @block.tensor
        def _(pe):
            def project(t, g, k):
                if g == 0:
                    pe.wait_ge(x_hi_done, G * t + k + 1)
                    pe.wait_ge(x_lo_done, G * t + k + 1)
                if k == 0:
                    wait(pe, q_lo_done, G * t + g)
                    if g == 4:
                        wait(pe, out_done, G * (t - 1) + 4)
                cols = slice(g * P, (g + 1) * P)
                nc.tensor.matmul(q_bank[:, :], wq_hi[:, k, cols], x_lo[:, k, :], start=k == 0, stop=False)
                nc.tensor.matmul(q_bank[:, :], wq_lo[:, k, cols], x_hi[:, k, :], start=False, stop=False)
                last = nc.tensor.matmul(q_bank[:, :], wq_hi[:, k, cols], x_hi[:, k, :],
                                        start=False, stop=k == G - 1)
                if k == G - 1:
                    last.then_inc(q_mm, 1)
                elif g == G - 1:
                    last.then_inc(x_used, 1)

            def bound(t, g, rt):
                if rt == 0:
                    pe.wait_ge(q_hi_done, G * t + g + 1)
                    pe.wait_ge(q_lo_done, G * t + g + 1)
                    if g == 0:
                        pe.wait_ge(kb_loaded, 16 * KB_DMAS * batches(t))
                wait(pe, bound_read, RT * (G * t + g) + rt - 1)
                bank, rows = a_bank[rt % 2], slice(rt * P, (rt + 1) * P)
                ip = slice(J * TEXT, J * KEYS)
                nc.tensor.matmul(bank[:, :], q_hi[:, g % 2, rows], kb[:, g, :], start=True, stop=False)
                nc.tensor.matmul(bank[:, ip], q_hi[:, g % 2, rows], kb_lo[:, g, :], start=False, stop=False)
                nc.tensor.matmul(bank[:, ip], q_lo[:, g % 2, rows], kb[:, g, ip],
                                 start=False, stop=True).then_inc(bound_mm, 1)

            def score(t, g, pair):
                if pair == 0:
                    pe.wait_ge(q_stacked[g], 3 * 16 * (t + 1))
                    pe.wait_ge(m_stacked[g], 16 * (t + 1))
                    if g == 0:
                        pe.wait_ge(kst_loaded, 16 * KST_DMAS * batches(t))
                wait(pe, exp_done, 2 * (G * t + g) + pair)
                for i in range(2):
                    j = 2 * pair + i
                    last = nc.tensor.matmul(s_bank[0:TEXT, i, :], kst[:, j, g, :], stack[0:STACK, g, j, :],
                                            start=True, stop=True)
                last.then_inc(score_mm, 1)

            def values(t, g):
                u = G * t + g
                if g == 0:
                    pe.wait_ge(v_loaded, 16 * V_DMAS * batches(t))
                pe.wait_ge(exp_done, 2 * u + 2)
                wait(pe, scaled_done, u)
                wait(pe, att_done, u)
                for j in range(J):
                    h = J * g + j
                    nc.tensor.matmul(pv_bank[j * DH:(j + 1) * DH, :], v_sb[:, h * DH:(h + 1) * DH],
                                     probs[:, j, :], start=True, stop=True)
                for j in range(J):
                    last = nc.tensor.matmul(l_bank[j * DH:(j + 1) * DH, :], ones[:, :], probs[:, j, :],
                                            start=True, stop=True)
                last.then_inc(pv_mm, 1)

            def ip_values(t, g):
                pe.wait_ge(sums_read, G * t + g + 1)
                pe.wait_ge(rows_copied, G * t + g + 3)
                if g == 0:
                    pe.wait_ge(vst_loaded, 16 * VST_DMAS * batches(t))
                nc.tensor.matmul(l_bank[:, :], vst[:, g, :], by_row[0:IPROWS, :], start=True, stop=True
                                 ).then_inc(ipv_mm, 1)

            def turn(t, g):
                u = G * t + g
                if runs(*earlier(t, g, 1)):
                    pe.wait_ge(bound_read, RT * u)
                if runs(*earlier(t, g, 3)):
                    pe.wait_ge(ip_p_done, u - 2)
                else:
                    pe.wait_ge(cleared, CLEARED)
                wait(pe, rows_copied, u - 1)
                if g == 3:
                    wait(pe, out_done, G * t)
                for rt in range(RT):
                    last = nc.tensor.transpose(t_bank[0:TURNED, rt * P:(rt + 1) * P], by_query[:, rt, :],
                                               idn[:, :])
                last.then_inc(turned, 1)

            def output(t):
                for m in range(G):
                    bank = q_bank if m % 2 else t_bank
                    if m == 0:
                        pe.wait_ge(rows_copied, G * (t + 1) + 2)
                    elif m == 1:
                        wait(pe, q_lo_done, no_more(G * (t + 1) + 4))
                    else:
                        pe.wait_ge(out_done, G * t + m - 1)
                    cols = slice(m * P, (m + 1) * P)
                    for k in range(G):
                        if m == 0:
                            pe.wait_ge(att_hi_done, G * t + k + 1)
                            pe.wait_ge(att_lo_done, G * t + k + 1)
                        nc.tensor.matmul(bank[:, :], wo_hi[:, k, cols], att_lo[:, k, :], start=k == 0, stop=False)
                        nc.tensor.matmul(bank[:, :], wo_lo[:, k, cols], att_hi[:, k, :], start=False, stop=False)
                        last = nc.tensor.matmul(bank[:, :], wo_hi[:, k, cols], att_hi[:, k, :],
                                                start=False, stop=k == G - 1)
                    last.then_inc(out_mm, 1)

            def iteration(t):
                for g in range(G):
                    now, a, s, c = (t, g), earlier(t, g, 1), earlier(t, g, 3), earlier(t, g, 4)
                    if runs(*s):
                        score(*s, 0)
                    if runs(*now):
                        project(*now, 0)
                        project(*now, 1)
                    if runs(*a):
                        bound(*a, 0)
                        bound(*a, 1)
                    if runs(*now):
                        project(*now, 2)
                    if runs(*s):
                        score(*s, 1)
                    if runs(*now):
                        project(*now, 3)
                    if runs(*c):
                        ip_values(*c)
                    if runs(*a):
                        bound(*a, 2)
                    if runs(*now):
                        project(*now, 4)
                    if runs(*a):
                        bound(*a, 3)
                    if g == 3 and runs(t - 1, 0):
                        output(t - 1)
                    if runs(*s):
                        values(*s)
                    if runs(*a) or runs(*s):
                        turn(t, g)

            over_tiles(pe, iteration)

        @block.scalar
        def _(act):
            def exps(t, g, pair):
                u = G * t + g
                act.wait_ge(score_mm, 2 * u + pair + 1)
                wait(act, pv_mm, u)
                nc.scalar.activation(probs[:, 2 * pair:2 * pair + 2, :], s_bank[0:TEXT, :, :], ACT.Exp,
                                     scale=SCALE).then_inc(exp_done, 1)

            def copy_rows(t, g):
                u = G * t + g
                act.wait_ge(turned, u)
                wait(act, ipv_mm, u - 3)
                tp, gp = earlier(t, g, 2)
                if runs(tp, gp):
                    act.wait_ge(m_stacked[gp], 16 * (tp + 1))
                nc.scalar.activation(by_row[:, :], t_bank[0:TURNED, :], ACT.Copy).then_inc(rows_copied, 1)

            def att_high(t, g):
                act.wait_ge(att_done, G * t + g + 1)
                wait(act, out_mm, G * t)
                nc.scalar.activation(att_hi[:, g, :], att[:, :], ACT.Copy).then_inc(att_hi_done, 1)

            def q_high(t, g):
                u = G * t + g
                act.wait_ge(q_mm, u + 1)
                lag = 1 if g == 0 else 2
                wait(act, bound_mm, RT * (u - lag + 1))
                tp, gp = earlier(t, g, lag)
                if runs(tp, gp):
                    act.wait_ge(q_stacked[gp], 3 * 16 * (tp + 1))
                nc.scalar.activation(q_hi[:, g % 2, :], q_bank[:, :], ACT.Copy).then_inc(q_hi_done, 1)

            def rough_reciprocal(t, g):
                u = G * t + g
                act.wait_ge(pv_mm, u + 1)
                wait(act, refined, u)
                nc.scalar.activation(rough[:, :], l_bank[:, :], ACT.Ln).then_inc(ln_done, 1)
                act.wait_ge(ln_done, u + 1)
                nc.scalar.activation(rough[:, :], rough[:, :], ACT.Exp, scale=-1.0).then_inc(rough_done, 1)

            def ip_exps(t, g):
                u = G * t + g
                act.wait_ge(ip_sub_done, u + 1)
                wait(act, ip_norm_done, u)
                nc.scalar.activation(ip_e[:, :, :], ip_x[:, :, :], ACT.Exp).then_inc(ip_exp_done, 1)

            def x_high(t, k):
                slot = snap(act, x_slot(t, k))
                act.wait_ge(x_loaded[k], 16 * (t + 1))
                if k < G - 1:
                    wait(act, x_used, (G - 1) * (t - 1) + k + 1)
                else:
                    wait(act, q_mm, G * t)
                nc.scalar.activation(x_hi[:, k, :], x_sb[:, bass.ds(slot, W)], ACT.Copy).then_inc(x_hi_done, 1)

            def iteration(t):
                for g in range(G):
                    now, a, s, c = (t, g), earlier(t, g, 1), earlier(t, g, 3), earlier(t, g, 4)
                    split = g == G - 1 and has_next(t)
                    if runs(*s):
                        exps(*s, 0)
                    if split:
                        x_high(t + 1, 0)
                    if runs(*s):
                        exps(*s, 1)
                    if split:
                        x_high(t + 1, 1)
                    if runs(*c):
                        att_high(*c)
                    if split:
                        x_high(t + 1, 2)
                        x_high(t + 1, 3)
                    if runs(*now):
                        q_high(*now)
                    if split:
                        x_high(t + 1, 4)
                    if runs(*s):
                        rough_reciprocal(*s)
                    if runs(*a) or runs(*s):
                        copy_rows(t, g)
                    if runs(*a):
                        ip_exps(*a)

            nc.scalar.preload_act_table_set("natural_log_exp_and_others")
            for k in range(G):
                x_high(0, k)
            iteration(0)
            with act.Fori(1, TILES - 1) as t:
                iteration(t)
            iteration(TILES - 1)
            iteration(TILES)

        @block.vector
        def _(dve):
            def read_bound(t, g, rt):
                u = G * t + g
                bank = a_bank[rt % 2]
                dve.wait_ge(bound_mm, RT * u + rt + 1)
                if rt == 0:
                    wait(dve, turned, u)
                    wait(dve, ip_sub_done, u)
                nc.vector.tensor_reduce(by_query[:, rt, IPROWS:TURNED],
                                        bank[:, 0:J * TEXT].rearrange("p (j n) -> p j n", j=J), AX_X, ALU.max,
                                        negate=True)
                row = mask[:, bass.ds(t * RT + rt, 1), :].to_broadcast([P, J, IP])
                nc.vector.scalar_tensor_tensor(
                    ip_s[:, rt * J:(rt + 1) * J, :],
                    bank[:, J * TEXT:J * KEYS].rearrange("p (j n) -> p j n", j=J),
                    SCALE, row, ALU.mult, ALU.add).then_inc(bound_read, 1)

            def ip_sums(t, g):
                u = G * t + g
                dve.wait_ge(ip_exp_done, u + 1)
                wait(dve, ip_rec_done, u)
                nc.vector.tensor_reduce(ip_sum[:, :], ip_e[:, :, :], AX_X, ALU.add).then_inc(ip_sum_done, 1)
                wait(dve, ip_norm_done, u)
                dve.wait_ge(ip_sum_done, u + 1)
                nc.vector.reciprocal(ip_rec[:, :], ip_sum[:, :]).then_inc(ip_rec_done, 1)

            def scale_values(t, g):
                u = G * t + g
                dve.wait_ge(rough_done, u + 1)
                wait(dve, att_lo_done, u)
                nc.vector.tensor_tensor(att[:, :], l_bank[:, :], rough[:, :], ALU.mult).then_inc(sums_read, 1)
                dve.wait_ge(sums_read, u + 1)
                nc.vector.scalar_tensor_tensor(att[:, :], att[:, :], 2.0, rough[:, :], ALU.subtract, ALU.mult,
                                               reverse0=True).then_inc(refined, 1)
                dve.wait_ge(refined, u + 1)
                nc.vector.tensor_tensor(att[:, :], pv_bank[:, :], att[:, :], ALU.mult).then_inc(scaled_done, 1)

            def add_ip(t, g):
                u = G * t + g
                dve.wait_ge(ipv_mm, u + 1)
                dve.wait_ge(scaled_done, u + 1)
                nc.vector.tensor_tensor(att[:, :], l_bank[:, :], att[:, :], ALU.add).then_inc(att_done, 1)

            def ip_shift(t, g):
                u = G * t + g
                dve.wait_ge(bound_read, RT * (u + 1))
                nc.vector.tensor_reduce(ip_max[:, :], ip_s[:, :, :], AX_X, ALU.max).then_inc(ip_max_done, 1)
                wait(dve, ip_exp_done, u)
                dve.wait_ge(ip_max_done, u + 1)
                nc.vector.tensor_tensor(ip_x[:, :, :], ip_s[:, :, :],
                                        ip_max[:, :].unsqueeze(2).to_broadcast([P, RT * J, IP]),
                                        ALU.subtract).then_inc(ip_sub_done, 1)

            def q_low(t, g):
                u = G * t + g
                dve.wait_ge(q_hi_done, u + 1)
                nc.vector.tensor_tensor(q_lo[:, g % 2, :], q_bank[:, :], q_hi[:, g % 2, :].bitcast(F32),
                                        ALU.subtract).then_inc(q_lo_done, 1)

            def finish(t):
                for m in range(G):
                    residual = x_sb[:, bass.ds(snap(dve, x_slot(t, m)), W)]
                    wait(dve, out_stored[m % 2], 16 * stores_before(t, m))
                    dve.wait_ge(out_mm, G * t + m + 1)
                    bank = q_bank if m % 2 else t_bank
                    nc.vector.scalar_tensor_tensor(out_sb[:, m % 2, :], bank[:, :], bias[:, m:m + 1], residual,
                                                   ALU.add, ALU.add).then_inc(out_done, 1)

            def iteration(t):
                for g in range(G):
                    now, a, i, c = (t, g), earlier(t, g, 1), earlier(t, g, 2), earlier(t, g, 4)
                    if runs(*c):
                        scale_values(*c)
                    if runs(*a):
                        read_bound(*a, 0)
                        read_bound(*a, 1)
                    if runs(*i):
                        ip_sums(*i)
                    if runs(*c):
                        add_ip(*c)
                    if runs(*a):
                        read_bound(*a, 2)
                        read_bound(*a, 3)
                        ip_shift(*a)
                    if runs(*now):
                        q_low(*now)
                    if g == 3 and runs(t - 1, 0):
                        finish(t - 1)

            nc.vector.memset(ones[:, :], 1.0).then_inc(cleared, 1)
            nc.vector.memset(by_query[:, :, :], 0.0).then_inc(cleared, 1)
            nc.vector.memset(kst[3 * DH:STACK, :, :, :].bitcast(F32), 1.0).then_inc(cleared, 1)
            over_tiles(dve, iteration)

        @block.gpsimd
        def _(pool):
            def ip_norm(t, g):
                u = G * t + g
                pool.wait_ge(ip_rec_done, u + 1)
                wait(pool, ip_p_done, u)
                nc.gpsimd.tensor_tensor(ip_n[:, :, :].rearrange("p r (j n) -> p (r j) n", j=J), ip_e[:, :, :],
                                        ip_rec[:, :].unsqueeze(2).to_broadcast([P, RT * J, IP]),
                                        ALU.mult).then_inc(ip_norm_done, 1)

            def ip_split(t, g):
                u = G * t + g
                pool.wait_ge(ip_norm_done, u + 1)
                pool.wait_ge(turned, u + 2)
                hi, lo, again = (by_query[:, :, i * J * IP:(i + 1) * J * IP] for i in range(3))
                unit = one[:, :].unsqueeze(2).to_broadcast([P, RT, J * IP])
                nc.gpsimd.tensor_tensor(hi.bitcast(F32R), ip_n[:, :, :], unit, ALU.mult).then_inc(ip_hi_done, 1)
                nc.gpsimd.tensor_tensor(again.bitcast(F32R), ip_n[:, :, :], unit, ALU.mult).then_inc(ip_hi_done, 1)
                pool.wait_ge(ip_hi_done, 2 * (u + 1))
                nc.gpsimd.tensor_tensor(lo.bitcast(F32R), ip_n[:, :, :], hi, ALU.subtract).then_inc(ip_p_done, 1)

            def att_low(t, g):
                pool.wait_ge(att_hi_done, G * t + g + 1)
                nc.gpsimd.tensor_tensor(att_lo[:, g, :], att[:, :], att_hi[:, g, :].bitcast(F32),
                                        ALU.subtract).then_inc(att_lo_done, 1)

            def x_low(t, k):
                place = x_sb[:, bass.ds(snap(pool, x_slot(t, k)), W)]
                pool.wait_ge(x_hi_done, G * t + k + 1)
                nc.gpsimd.tensor_tensor(x_lo[:, k, :], place, x_hi[:, k, :].bitcast(F32),
                                        ALU.subtract).then_inc(x_lo_done, 1)

            def iteration(t):
                for g in range(G):
                    i, s, c = earlier(t, g, 2), earlier(t, g, 3), earlier(t, g, 4)
                    split = g == G - 1 and has_next(t)
                    if runs(*s):
                        ip_split(*s)
                    if split:
                        x_low(t + 1, 0)
                    if runs(*i):
                        ip_norm(*i)
                    if split:
                        x_low(t + 1, 1)
                    if runs(*c):
                        att_low(*c)
                    if split:
                        for k in range(2, G):
                            x_low(t + 1, k)

            nc.gpsimd.memset(kb[:, :, :].bitcast(F32), 0.0).then_inc(cleared, 1)
            nc.gpsimd.memset(kb_lo[:, :, :].bitcast(F32), 0.0).then_inc(cleared, 1)
            nc.gpsimd.memset(vst[:, :, :].bitcast(F32), 0.0).then_inc(cleared, 1)
            nc.gpsimd.memset(one[:, :], 1.0).then_inc(cleared, 1)
            pool.wait_ge(cleared, CLEARED)
            for k in range(G):
                x_low(0, k)
            iteration(0)
            with pool.Fori(1, TILES - 1) as t:
                iteration(t)
            iteration(TILES - 1)
            iteration(TILES)


def kernel(**inputs):
    import concourse.bacc as bacc
    from concourse.bass_utils import run_bass_kernel_spmd

    def a(name):
        return np.asarray(inputs[name])

    def by_feature(w):
        return np.ascontiguousarray(w.reshape(w.shape[0], G, J, DH).transpose(0, 1, 3, 2).reshape(w.shape[0], D))

    xs = np.linspace(0.0, 1.0, GRID_W, dtype=np.float32)
    ys = np.linspace(0.0, 1.0, GRID_H, dtype=np.float32)
    token = np.arange(S).reshape(S // P, P)
    gx = xs[token[0] % GRID_W].reshape(P, 1)
    gy = np.repeat(ys[token // GRID_W].T[:, None, :], B * BOXES, axis=1)

    c = a("ctx_2048")
    arrays = {
        "xT": np.ascontiguousarray(a("x").reshape(B * S, D).T),
        "ctxT": np.ascontiguousarray(np.concatenate([c[:, :TEXT].reshape(B * TEXT, C), c[:, TEXT:].reshape(B * IP, C)]).T),
        "boxes": a("fside_Bx4x4_0").reshape(1, B * BOXES * 4),
        "gx": gx, "gy": np.ascontiguousarray(gy),
        "ident": np.eye(P, dtype=np.float32),
        "wq": by_feature(a("L0_xattn_w_q")),
        "wk": by_feature(a("L0_xattn_w_k")),
        "wv": a("L0_xattn_w_v"),
        "wkip": by_feature(a("L0_xattn_w_k_ip")),
        "wvip": a("L0_xattn_w_v_ip"),
        "wo": a("L0_xattn_w_out"),
        "bo": np.ascontiguousarray(a("L0_xattn_b_out").reshape(G, P).T.reshape(D)),
    }
    nc = bacc.Bacc("TRN2", target_bir_lowering=False, num_devices=1)
    args = [nc.dram_tensor(n, v.shape, mybir.dt.from_np(v.dtype), kind="ExternalInput").ap()
            for n, v in arrays.items()]
    args.append(nc.dram_tensor("outT", (D, B * S), F32, kind="ExternalOutput").ap())
    xattn_kernel(nc, *args)
    r = run_bass_kernel_spmd(nc, [arrays], core_ids=[0])
    return np.ascontiguousarray(r.results[0]["outT"].T).reshape(B, S, D)
```

```python
from contextlib import ExitStack

import numpy as np

import concourse.bass as bass
from concourse import mybir

F32 = mybir.dt.float32
F32R = mybir.dt.float32r
ALU = mybir.AluOpType
ACT = mybir.ActivationFunctionType
AX_X = mybir.AxisListType.X

P = 128
B, S, D, C = 4, 2048, 640, 1024
HEADS, DH = 20, 32
KEYS, TEXT, IP = 128, 120, 8
BOXES = 4
W = 512
J = P // DH
G = HEADS // J
RT = W // P
TILES = B * S // W
TPB = S // W
CK = C // P
NEG = -10000.0
SCALE = float(DH) ** -0.5
STACK = 3 * DH + 1
IPROWS = 3 * J * IP
TURNED = IPROWS + J
GRID_W, GRID_H = 64, 32
assert GRID_W * GRID_H == S


def wait(engine, sem, value):
    if isinstance(value, int) and value <= 0:
        return
    engine.wait_ge(sem, value)


def snap(engine, value):
    return value if isinstance(value, int) else engine.snap(value)


def xattn_kernel(nc, xT, ctxT, boxes, gx, gy, ident, wq, wk, wv, wkip, wvip, wo, bo, outT):
    def scratch(name, shape, dt):
        return nc.dram_tensor(name, shape, dt, kind="Internal").ap()

    kt_hi_d = scratch("kt_hi_d", (P, G, B, KEYS), F32)
    kt_lo_d = scratch("kt_lo_d", (P, G, B, KEYS), F32)
    v_d = scratch("v_d", (B, TEXT, D), F32)
    vip_hi_d = scratch("vip_hi_d", (B, IP, D), F32)
    vip_lo_d = scratch("vip_lo_d", (B, IP, D), F32)

    with ExitStack() as ctx:
        def sb(name, shape, dt=F32, where=None):
            return (where or ctx).enter_context(nc.sbuf_tensor(name, shape, dt))

        def sem(name):
            return ctx.enter_context(nc.semaphore(name))

        wq_hi = sb("wq_hi", [P, G, D], F32R)
        wq_lo = sb("wq_lo", [P, G, D], F32R)
        wo_hi = sb("wo_hi", [P, G, D], F32R)
        wo_lo = sb("wo_lo", [P, G, D], F32R)
        bias = sb("bias", [P, G])
        idn = sb("idn", [P, P])
        mask = sb("mask", [P, TILES * RT, IP])
        x_sb = sb("x_sb", [P, 2 * G * W])
        kb = sb("kb", [P, G, J * KEYS], F32R)
        kb_lo = sb("kb_lo", [P, G, J * IP], F32R)
        kb_cleared = sem("kb_cleared")
        v_stored = sem("v_stored")
        x_loaded = [sem(f"x_loaded{k}") for k in range(G)]

        keys_and_values(nc, ctx, sb, sem, xT, x_sb, x_loaded, kb, kb_lo, kb_cleared, v_stored,
                        ctxT, boxes, gx, gy, ident, wq, wk, wv, wkip, wvip, wo, bo,
                        wq_hi, wq_lo, wo_hi, wo_lo, bias, idn, mask,
                        kt_hi_d, kt_lo_d, v_d, vip_hi_d, vip_lo_d)
        attention(nc, ctx, sb, sem, xT, x_sb, x_loaded, kb, kb_lo, kb_cleared, v_stored, outT,
                  wq_hi, wq_lo, wo_hi, wo_lo, bias, idn, mask,
                  kt_hi_d, kt_lo_d, v_d, vip_hi_d, vip_lo_d)


def keys_and_values(nc, ctx, sb, sem, xT, x_sb, x_loaded, kb, kb_lo, kb_cleared, v_stored,
                    ctxT, boxes, gx, gy, ident, wq, wk, wv, wkip, wvip, wo, bo,
                    wq_hi, wq_lo, wo_hi, wo_lo, bias, idn, mask,
                    kt_hi_d, kt_lo_d, v_d, vip_hi_d, vip_lo_d):
    HALF = D // 2
    ALL_TEXT, ALL_IP = B * TEXT, B * IP
    V_FILLS = 2 * B
    G_LEFT = (G + 1) // 2
    IP_PARTS = (slice(0, G_LEFT * P), slice(G_LEFT * P, D))
    assert B * D <= G * W
    with ExitStack() as temp:
        ctx_sb = sb("ctx_sb", [P, CK, B * KEYS], F32, temp)
        w_a = sb("w_a", [P, CK, D], F32, temp)
        w_b = sb("w_b", [P, CK, D], F32, temp)
        w_c = sb("w_c", [P, CK, D], F32, temp)
        w_raw = sb("w_raw", [P, G, D], F32, temp)
        kt_hi = sb("kt_hi", [P, G, B, KEYS], F32R, temp)
        kt_lo = sb("kt_lo", [P, G, B, KEYS], F32R, temp)
        v_sb = x_sb[0:TEXT, G * W:G * W + B * D].rearrange("p (b n) -> p b n", b=B)
        k_ip = sb("k_ip", [2 * ALL_IP, G_LEFT * P], F32, temp)
        vip_hi = sb("vip_hi", [P, G_LEFT * P], F32R, temp)
        vip_lo = sb("vip_lo", [P, G_LEFT * P], F32R, temp)
        box = sb("box", [P, B, BOXES * 4], F32, temp)
        grid_x = sb("grid_x", [P, 1], F32, temp)
        grid_y = sb("grid_y", [P, S // P], F32, temp)
        inside = sb("inside", [P, B, S // P, BOXES], F32, temp)
        test_x = sb("test_x", [P, B, BOXES, 2], F32, temp)
        test_y = sb("test_y", [P, 2, S // P], F32, temp)
        anybox = sb("anybox", [P, B, S // P], F32, temp)
        k_bank = [temp.enter_context(nc.psum_tensor(f"k_bank{g}", [P, W], F32)) for g in range(G)]
        spare = [temp.enter_context(nc.psum_tensor(f"kv_bank{i}", [P, W], F32)) for i in range(8 - G)]
        ip_bank, turn_bank = k_bank[1], k_bank[2]
        v_bank = [*spare, k_bank[0], k_bank[3], k_bank[4], *spare[0:2]]
        EARLY_FILLS = len(spare) + 1

        raw_loaded = [sem("wq_loaded"), sem("wo_loaded")]
        small_loaded = sem("small_loaded")
        chunk_loaded = [sem(f"chunk_loaded{k}") for k in range(CK)]
        w_loaded = {n: sem(f"{n}_loaded") for n in ("wkip", "wv", "wvip")}
        key_mm, key_hi, key_lo = sem("key_mm"), sem("key_hi"), sem("key_lo")
        value_mm, value_read = sem("value_mm"), sem("value_read")
        ip_mm, k_ip_copied, k_ip_turned = sem("ip_mm"), sem("k_ip_copied"), sem("k_ip_turned")
        v_ip_hi, v_ip_lo = sem("v_ip_hi"), sem("v_ip_lo")
        raw_hi = sem("raw_hi")
        raw_lo = sem("raw_lo")
        mask_step = sem("mask_step")
        stored = sem("kv_stored")

        def turned_groups(bank):
            both = bank[:, 0:G_LEFT * 2 * ALL_IP].rearrange("p (g h n) -> p g h n", g=G_LEFT, h=2)
            left, right = both[:, :, 0, :], both[:, 0:G - G_LEFT, 1, :]
            return [side.rearrange("p g (b n) -> p g b n", b=B) for side in (left, right)]

        def by_batch(bank):
            return bank[:, 0:ALL_TEXT].rearrange("p (b n) -> p b n", b=B)

        with nc.Block() as block:
            @block.sync
            def _(sp):
                for k in range(CK):
                    rows = slice(k * P, (k + 1) * P)
                    sp.dma_start(ctx_sb[:, k, :], ctxT[rows, :]).then_inc(chunk_loaded[k], 16)
                    sp.dma_start(w_a[:, k, :], wk[rows, :]).then_inc(chunk_loaded[k], 16)
                sp.dma_start(w_c[:, :, :], wv.rearrange("(k p) n -> p k n", p=P)).then_inc(w_loaded["wv"], 16)
                sp.dma_start(idn[:, :], ident).then_inc(small_loaded, 16)
                sp.dma_start(bias[:, :], bo.rearrange("(p g) -> p g", g=G)).then_inc(small_loaded, 16)
                sp.dma_start(grid_x[:, :], gx).then_inc(small_loaded, 16)
                sp.dma_start(grid_y[:, :], gy).then_inc(small_loaded, 16)
                sp.dma_start(box[:, :, :].rearrange("p b n -> p (b n)"),
                             boxes.to_broadcast([P, B * BOXES * 4])).then_inc(small_loaded, 16)
                sp.dma_start(w_raw[:, :, :], wq.rearrange("(k p) n -> p k n", p=P)).then_inc(raw_loaded[0], 16)
                sp.dma_start(w_b[:, :, :], wkip.rearrange("(k p) n -> p k n", p=P)).then_inc(w_loaded["wkip"], 16)
                sp.wait_ge(key_mm, G)
                sp.dma_start(w_a[:, :, :], wvip.rearrange("(k p) n -> p k n", p=P)).then_inc(w_loaded["wvip"], 16)
                for k in range(G):
                    sp.dma_start(x_sb[:, k * W:(k + 1) * W], xT[k * P:(k + 1) * P, 0:W]).then_inc(x_loaded[k], 16)
                sp.wait_ge(raw_hi, 1)
                sp.wait_ge(raw_lo, 1)
                sp.dma_start(w_raw[:, :, :], wo.rearrange("(k p) n -> p k n", p=P)).then_inc(raw_loaded[1], 16)
                sp.wait_ge(key_hi, G + 2)
                sp.dma_start(kt_hi_d, kt_hi[:, :, :, :].bitcast(F32)).then_inc(stored, 16)
                sp.wait_ge(key_lo, G + 2)
                sp.dma_start(kt_lo_d, kt_lo[:, :, :, :].bitcast(F32)).then_inc(stored, 16)
                for part, sem_made, dst in ((vip_hi, v_ip_hi, vip_hi_d), (vip_lo, v_ip_lo, vip_lo_d)):
                    sp.wait_ge(sem_made, 1)
                    for i, cols in enumerate(IP_PARTS):
                        rows = slice((2 + i) * ALL_IP, (3 + i) * ALL_IP)
                        sp.dma_start(dst.rearrange("b k n -> (b k) n")[:, cols],
                                     part[rows, 0:cols.stop - cols.start].bitcast(F32)).then_inc(stored, 16)
                for b in range(B):
                    sp.wait_ge(value_read, 2 * (b + 1))
                    sp.dma_start(v_d[b, :, :], v_sb[:, b, :]).then_inc(v_stored, 16)
                sp.wait_ge(stored, 6 * 16)

            @block.tensor
            def _(pe):
                def value(n):
                    b, half = n // 2, n % 2
                    for k in range(CK):
                        last = nc.tensor.matmul(v_bank[n][0:TEXT, 0:HALF], ctx_sb[:, k, b * TEXT:(b + 1) * TEXT],
                                                w_c[:, k, half * HALF:(half + 1) * HALF],
                                                start=k == 0, stop=k == CK - 1)
                    last.then_inc(value_mm, 1)

                for k in range(CK):
                    pe.wait_ge(chunk_loaded[k], 2 * 16)
                    for g in range(G):
                        mm = nc.tensor.matmul(k_bank[g][:, 0:ALL_TEXT], w_a[:, k, g * P:(g + 1) * P],
                                              ctx_sb[:, k, 0:ALL_TEXT], start=k == 0, stop=k == CK - 1)
                        if k == CK - 1:
                            mm.then_inc(key_mm, 1)
                pe.wait_ge(w_loaded["wv"], 16)
                for n in range(EARLY_FILLS):
                    if n == EARLY_FILLS - 1:
                        pe.wait_ge(key_hi, G)
                        pe.wait_ge(key_lo, G)
                    value(n)
                pe.wait_ge(w_loaded["wkip"], 16)
                pe.wait_ge(w_loaded["wvip"], 16)
                for k in range(CK):
                    for i, (w, cols) in enumerate((w, cols) for w in (w_b, w_a) for cols in IP_PARTS):
                        last = nc.tensor.matmul(ip_bank[i * ALL_IP:(i + 1) * ALL_IP, 0:cols.stop - cols.start],
                                                ctx_sb[:, k, ALL_TEXT:], w[:, k, cols],
                                                start=k == 0, stop=k == CK - 1)
                last.then_inc(ip_mm, 1)
                value(EARLY_FILLS)
                pe.wait_ge(small_loaded, 5 * 16)
                pe.wait_ge(k_ip_copied, 1)
                for g in range(G_LEFT):
                    sides = 2 if g < G - G_LEFT else 1
                    last = nc.tensor.transpose(turn_bank[:, g * 2 * ALL_IP:(g * 2 + sides) * ALL_IP],
                                               k_ip[0:sides * ALL_IP, g * P:(g + 1) * P],
                                               idn[0:sides * ALL_IP, 0:sides * ALL_IP])
                last.then_inc(k_ip_turned, 1)
                for n in range(EARLY_FILLS + 1, V_FILLS):
                    if n > EARLY_FILLS + 1:
                        pe.wait_ge(value_read, n - EARLY_FILLS - 1)
                    value(n)

            @block.scalar
            def _(act):
                def split_raw(i, hi):
                    act.wait_ge(raw_loaded[i], 16)
                    nc.scalar.activation(hi[:, :, :], w_raw[:, :, :], ACT.Copy).then_inc(raw_hi, 1)

                nc.scalar.preload_act_table_set("natural_log_exp_and_others")
                for g in range(G):
                    act.wait_ge(key_mm, g + 1)
                    nc.scalar.activation(kt_hi[:, g, :, 0:TEXT], by_batch(k_bank[g]),
                                         ACT.Copy).then_inc(key_hi, 1)
                split_raw(0, wq_hi)
                for n in range(V_FILLS):
                    if n == EARLY_FILLS:
                        act.wait_ge(ip_mm, 1)
                        for i in range(2):
                            width = IP_PARTS[i].stop - IP_PARTS[i].start
                            rows = slice(i * ALL_IP, (i + 1) * ALL_IP)
                            copied = nc.scalar.activation(k_ip[rows, 0:width], ip_bank[rows, 0:width], ACT.Copy)
                        copied.then_inc(k_ip_copied, 1)
                        for i in (2, 3):
                            width = IP_PARTS[i - 2].stop - IP_PARTS[i - 2].start
                            rows = slice(i * ALL_IP, (i + 1) * ALL_IP)
                            made = nc.scalar.activation(vip_hi[rows, 0:width], ip_bank[rows, 0:width], ACT.Copy)
                        made.then_inc(v_ip_hi, 1)
                    act.wait_ge(value_mm, n + 1)
                    half = n % 2
                    nc.scalar.activation(v_sb[:, n // 2, half * HALF:(half + 1) * HALF],
                                         v_bank[n][0:TEXT, 0:HALF], ACT.Copy).then_inc(value_read, 1)
                    if n == EARLY_FILLS:
                        act.wait_ge(k_ip_turned, 1)
                        left, right = turned_groups(turn_bank)
                        nc.scalar.activation(kt_hi[:, 0:G_LEFT, :, TEXT:], left, ACT.Copy).then_inc(key_hi, 1)
                        nc.scalar.activation(kt_hi[:, G_LEFT:G, :, TEXT:], right, ACT.Copy).then_inc(key_hi, 1)
                    if n == EARLY_FILLS + 1:
                        split_raw(1, wo_hi)

            @block.vector
            def _(dve):
                steps = 0

                def step(instruction):
                    nonlocal steps
                    steps += 1
                    instruction.then_inc(mask_step, 1)
                    dve.wait_ge(mask_step, steps)

                def split_raw(i, hi, lo):
                    dve.wait_ge(raw_loaded[i], 16)
                    dve.wait_ge(raw_hi, i + 1)
                    nc.vector.tensor_tensor(lo[:, :, :], w_raw[:, :, :], hi[:, :, :].bitcast(F32),
                                            ALU.subtract).then_inc(raw_lo, 1)

                dve.wait_ge(small_loaded, 5 * 16)
                bv = box[:, :, :].rearrange("p b (m c) -> p b m c", m=BOXES)
                nc.vector.tensor_scalar(test_x[:, :, :, 0], bv[:, :, :, 0], grid_x[:, 0:1], None, ALU.is_le)
                step(nc.vector.tensor_scalar(test_x[:, :, :, 1], bv[:, :, :, 2], grid_x[:, 0:1], None, ALU.is_ge))
                step(nc.vector.tensor_tensor(test_x[:, :, :, 0], test_x[:, :, :, 0], test_x[:, :, :, 1], ALU.mult))
                for b in range(B):
                    for m in range(BOXES):
                        nc.vector.tensor_scalar(test_y[:, 0, :], grid_y[:, :], bv[:, b, m, 1:2],
                                                test_x[:, b, m, 0:1], ALU.is_ge, ALU.mult)
                        step(nc.vector.tensor_scalar(test_y[:, 1, :], grid_y[:, :], bv[:, b, m, 3:4],
                                                     None, ALU.is_le))
                        step(nc.vector.tensor_tensor(inside[:, b, :, m], test_y[:, 0, :], test_y[:, 1, :],
                                                     ALU.mult))
                step(nc.vector.tensor_reduce(anybox[:, :, :], inside[:, :, :, :], AX_X, ALU.max))
                rows = mask[:, :, :].rearrange("p (b r) k -> p b r k", b=B)
                for m in range(BOXES):
                    nc.vector.tensor_scalar(rows[:, :, :, m], anybox[:, :, :], NEG, None, ALU.mult)
                step(nc.vector.tensor_scalar(rows[:, :, :, BOXES:IP], inside[:, :, :, :], -NEG, NEG,
                                             ALU.mult, ALU.add))
                for g in range(G):
                    dve.wait_ge(key_hi, g + 1)
                    nc.vector.tensor_tensor(kt_lo[:, g, :, 0:TEXT], by_batch(k_bank[g]),
                                            kt_hi[:, g, :, 0:TEXT].bitcast(F32), ALU.subtract).then_inc(key_lo, 1)
                split_raw(0, wq_hi, wq_lo)
                dve.wait_ge(v_ip_hi, 1)
                for i in (2, 3):
                    width = IP_PARTS[i - 2].stop - IP_PARTS[i - 2].start
                    rows = slice(i * ALL_IP, (i + 1) * ALL_IP)
                    made = nc.vector.tensor_tensor(vip_lo[rows, 0:width], ip_bank[rows, 0:width],
                                                   vip_hi[rows, 0:width].bitcast(F32), ALU.subtract)
                made.then_inc(v_ip_lo, 1)
                dve.wait_ge(key_hi, G + 2)
                for groups, turned in zip((slice(0, G_LEFT), slice(G_LEFT, G)), turned_groups(turn_bank)):
                    nc.vector.tensor_tensor(kt_lo[:, groups, :, TEXT:], turned,
                                            kt_hi[:, groups, :, TEXT:].bitcast(F32), ALU.subtract
                                            ).then_inc(key_lo, 1)
                split_raw(1, wo_hi, wo_lo)

            @block.gpsimd
            def _(pool):
                nc.gpsimd.memset(kb[:, :, :].bitcast(F32), 0.0).then_inc(kb_cleared, 1)
                nc.gpsimd.memset(kb_lo[:, :, :].bitcast(F32), 0.0).then_inc(kb_cleared, 1)


def attention(nc, ctx, sb, sem, xT, x_sb, x_loaded, kb, kb_lo, kb_cleared, v_stored, outT,
              wq_hi, wq_lo, wo_hi, wo_lo, bias, idn, mask,
              kt_hi_d, kt_lo_d, v_d, vip_hi_d, vip_lo_d):
    out_sb = sb("out_sb", [P, 2, W])
    x_hi = sb("x_hi", [P, G, W], F32R)
    x_lo = sb("x_lo", [P, G, W], F32R)
    q_hi = sb("q_hi", [P, 2, W], F32R)
    q_lo = sb("q_lo", [P, 2, W], F32R)
    stack = sb("stack", [P, G, J, W], F32R)
    probs = sb("probs", [TEXT, J, W])
    att = sb("att", [P, W])
    att_hi = sb("att_hi", [P, G, W], F32R)
    att_lo = sb("att_lo", [P, G, W], F32R)
    rough = sb("rough", [P, W])
    ip_s = sb("ip_s", [P, RT * J, IP])
    ip_x = sb("ip_x", [P, RT * J, IP])
    ip_e = sb("ip_e", [P, RT * J, IP])
    ip_n = sb("ip_n", [P, RT, J * IP])
    ip_max = sb("ip_max", [P, RT * J])
    ip_sum = sb("ip_sum", [P, RT * J])
    ip_rec = sb("ip_rec", [P, RT * J])
    by_query = sb("by_query", [P, RT, TURNED])
    by_row = sb("by_row", [TURNED, W], F32R)
    one = sb("one", [P, 1])
    ones = sb("ones", [TEXT, DH])
    kst = sb("kst", [STACK, J, G, TEXT], F32R)
    v_sb = sb("v_now", [TEXT, D])
    vst = sb("vst", [IPROWS, G, P], F32R)

    def psum(name):
        return ctx.enter_context(nc.psum_tensor(name, [P, W], F32))

    q_bank = psum("q_bank")
    a_bank = [psum(f"a_bank{i}") for i in range(2)]
    s_bank = ctx.enter_context(nc.psum_tensor("s_bank", [P, 2, W], F32))
    pv_bank = psum("pv_bank")
    l_bank = psum("l_bank")
    t_bank = psum("t_bank")

    out_stored = [sem(f"out_stored{i}") for i in range(2)]
    q_stacked = [sem(f"q_stacked{g}") for g in range(G)]
    m_stacked = [sem(f"m_stacked{g}") for g in range(G)]
    kb_loaded = [sem(f"kb_loaded{part}") for part in range(2)]
    kst_loaded = [sem(f"kst_loaded{part}") for part in range(2)]
    v_loaded = sem("v_loaded")
    vst_loaded = sem("vst_loaded")
    q_mm, bound_mm, score_mm, pv_mm = sem("q_mm"), sem("bound_mm"), sem("score_mm"), sem("pv_mm")
    ipv_mm, turned, out_mm, x_used = sem("ipv_mm"), sem("turned"), sem("out_mm"), sem("x_used")
    q_hi_done, exp_done, rows_copied = sem("q_hi_done"), sem("exp_done"), sem("rows_copied")
    ln_done, rough_done = sem("ln_done"), sem("rough_done")
    ip_exp_done, att_hi_done, x_hi_done = sem("ip_exp_done"), sem("att_hi_done"), sem("x_hi_done")
    q_lo_done, bound_read = sem("q_lo_done"), sem("bound_read")
    sums_read, refined = sem("sums_read"), sem("refined")
    scaled_done, att_done, out_done = sem("scaled_done"), sem("att_done"), sem("out_done")
    ip_max_done, ip_sub_done = sem("ip_max_done"), sem("ip_sub_done")
    ip_sum_done, ip_rec_done = sem("ip_sum_done"), sem("ip_rec_done")
    cleared, ip_norm_done, ip_hi_done = sem("cleared"), sem("ip_norm_done"), sem("ip_hi_done")
    ip_p_done, att_lo_done, x_lo_done = sem("ip_p_done"), sem("att_lo_done"), sem("x_lo_done")

    UNITS = TILES * G
    CLEARED = 5
    PARTS = (slice(0, 3), slice(3, G))
    KB_FIRST, KST_FIRST = (J, J), (2, 1)
    KB_DMAS, KST_DMAS, V_DMAS, VST_DMAS = 2 * J, [3 * (p.stop - p.start) for p in PARTS], 1, 3 * J

    def earlier(t, g, lag):
        return (t, g - lag) if g >= lag else (t - 1, g - lag + G)

    def no_more(count):
        return min(count, UNITS) if isinstance(count, int) else count

    def stores_before(t, m):
        return t * len(range(m % 2, G, 2)) + m // 2

    def x_slot(t, k):
        return (t % 2) * (G * W) + k * W

    def runs(t, g):
        return not isinstance(t, int) or 0 <= t < TILES

    def has_next(t):
        return not isinstance(t, int) or t < TILES - 1

    def batches(t):
        return t // TPB + 1

    def project_bank(t, g):
        return pv_bank if isinstance(t, int) and (t, g) == (0, 1) else q_bank

    def last_bank(m):
        return (q_bank[:, :], a_bank[0][:, :], a_bank[1][:, :], t_bank[:, :], s_bank[:, 0, :])[m]

    def over_tiles(engine, iteration):
        iteration(0)
        with engine.Fori(1, TILES) as t:
            iteration(t)
        iteration(TILES)

    with nc.Block() as block:

        @block.sync
        def _(sp):
            def load_x(t, k):
                column = snap(sp, t * W)
                slot = snap(sp, x_slot(t, k))
                wait(sp, out_done, G * (t - 2) + k + 1)
                sp.dma_start(x_sb[:, bass.ds(slot, W)],
                             xT[k * P:(k + 1) * P, bass.ds(column, W)]).then_inc(x_loaded[k], 16)

            def store(t, m):
                column = snap(sp, t * W)
                sp.wait_ge(out_done, G * t + m + 1)
                sp.dma_start(outT[m * P:(m + 1) * P, bass.ds(column, W)],
                             out_sb[:, m % 2, :]).then_inc(out_stored[m % 2], 16)

            def load_kb(b, part):
                groups = PARTS[part]
                wait(sp, bound_mm, RT * (G * (TPB * b - 1) + groups.stop))
                for j in range(J):
                    rows = slice(j, P, J)
                    sp.dma_start(kb[rows, groups, j * KEYS:(j + 1) * KEYS].bitcast(F32),
                                 kt_hi_d[rows, groups, b, :]).then_inc(kb_loaded[part], 16)
                    sp.dma_start(kb_lo[rows, groups, j * IP:(j + 1) * IP].bitcast(F32),
                                 kt_lo_d[rows, groups, b, TEXT:]).then_inc(kb_loaded[part], 16)

            def load_first_kb():
                for j in range(J):
                    rows = slice(j, P, J)
                    sp.dma_start(kb[rows, :, j * KEYS:(j + 1) * KEYS].bitcast(F32),
                                 kt_hi_d[rows, :, 0, :]).then_inc(kb_loaded[0], 16)
                    sp.dma_start(kb_lo[rows, :, j * IP:(j + 1) * IP].bitcast(F32),
                                 kt_lo_d[rows, :, 0, TEXT:]).then_inc(kb_loaded[1], 16)

            def load_first_kst():
                for i, (src, part) in enumerate(((kt_hi_d, 0), (kt_hi_d, 0), (kt_lo_d, 1))):
                    sp.dma_start(kst[i * DH:(i + 1) * DH, :, :, :].bitcast(F32).rearrange("r j g n -> r (j g) n"),
                                 src[:, :, 0, 0:TEXT]).then_inc(kst_loaded[part], 16)

            def load_kst(b, part):
                groups = PARTS[part]
                wait(sp, score_mm, 2 * (G * (TPB * b - 1) + groups.stop))
                for i, src in enumerate((kt_hi_d, kt_hi_d, kt_lo_d)):
                    for g in range(groups.start, groups.stop):
                        sp.dma_start(kst[i * DH:(i + 1) * DH, :, g, :].bitcast(F32), src[:, g, b, 0:TEXT]
                                     ).then_inc(kst_loaded[part], 16)

            def load_v(b):
                wait(sp, pv_mm, G * TPB * b)
                sp.dma_start(v_sb[:, :], v_d[b, :, :]).then_inc(v_loaded, 16)

            def load_vst(b, j):
                wait(sp, ipv_mm, G * TPB * b)
                for i, src in enumerate((vip_hi_d, vip_hi_d, vip_lo_d)):
                    at = (i * J + j) * IP
                    sp.dma_start(vst[at:at + IP, :, j * DH:(j + 1) * DH].bitcast(F32),
                                 src[b, :, :].rearrange("k (g n) -> k g n", g=G)[:, :, j * DH:(j + 1) * DH]
                                 ).then_inc(vst_loaded, 16)

            def iteration(t, batch=None, next_batch=None):
                front = runs(t, 0)
                first = isinstance(t, int) and t == 0
                later = batch is not None and not first
                for g in range(G):
                    if later and g == 3:
                        load_v(batch)
                    if front:
                        for i, (src, made) in enumerate(((q_hi, q_hi_done), (q_lo, q_lo_done), (q_hi, q_hi_done))):
                            if i < 2:
                                sp.wait_ge(made, G * t + g + 1)
                            sp.dma_start(stack[i * DH:(i + 1) * DH, g, :, :].bitcast(F32), src[:, g % 2, :].bitcast(F32)
                                         ).then_inc(q_stacked[g], 16)
                    if first and g == 3:
                        load_vst(batch, 3)
                    if g == 3:
                        for m in range(G):
                            if runs(t - 1, 0):
                                store(t - 1, m)
                            if front and has_next(t):
                                load_x(t + 1, m)
                            if later and m < J:
                                load_vst(batch, m)
                    ta, ga = earlier(t, g, 1)
                    if runs(ta, ga):
                        sp.wait_ge(rows_copied, G * t + g)
                        sp.dma_start(stack[3 * DH:STACK, ga, :, :].bitcast(F32),
                                     by_row[IPROWS:TURNED, :].bitcast(F32)).then_inc(m_stacked[ga], 16)
                    if g == 4 and next_batch is not None:
                        load_kb(next_batch, 0)
                    if later and g == 0:
                        load_kst(batch, 0)
                    if later and g == 1:
                        load_kb(batch, 1)
                    if later and g == 3:
                        load_kst(batch, 1)
                    if first and g == 0:
                        load_first_kst()
                    if first and g == 1:
                        load_v(batch)
                        sp.wait_ge(cleared, CLEARED)
                        load_vst(batch, 0)
                    if first and g == 2:
                        load_vst(batch, 1)
                        load_vst(batch, 2)
            sp.wait_ge(kb_cleared, 2)
            load_first_kb()
            sp.wait_ge(v_stored, 16 * B)
            iteration(0, batch=0)
            with sp.Fori(0, B - 1) as b:
                for i in range(1, TPB + 1):
                    iteration(b * TPB + i, batch=b + 1 if i == TPB else None,
                              next_batch=b + 1 if i == TPB - 1 else None)
            for t in range((B - 1) * TPB + 1, TILES + 1):
                iteration(t)
            for i in range(2):
                sp.wait_ge(out_stored[i], 16 * stores_before(TILES, i))

        @block.tensor
        def _(pe):
            def project(t, g, k):
                if g == 0:
                    pe.wait_ge(x_hi_done, G * t + k + 1)
                    pe.wait_ge(x_lo_done, G * t + k + 1)
                if k == 0:
                    before = {1: 0, 2: 1}.get(g, g) if isinstance(t, int) and t == 0 else g
                    wait(pe, q_lo_done, G * t + before)
                    if g == 4:
                        wait(pe, out_done, G * (t - 1) + 4)
                cols = slice(g * P, (g + 1) * P)
                bank = project_bank(t, g)
                nc.tensor.matmul(bank[:, :], wq_hi[:, k, cols], x_lo[:, k, :], start=k == 0, stop=False)
                nc.tensor.matmul(bank[:, :], wq_lo[:, k, cols], x_hi[:, k, :], start=False, stop=False)
                last = nc.tensor.matmul(bank[:, :], wq_hi[:, k, cols], x_hi[:, k, :],
                                        start=False, stop=k == G - 1)
                if k == G - 1:
                    last.then_inc(q_mm, 1)
                elif g == G - 1:
                    last.then_inc(x_used, 1)

            def bound(t, g, rt):
                if rt == 0:
                    pe.wait_ge(q_hi_done, G * t + g + 1)
                    pe.wait_ge(q_lo_done, G * t + g + 1)
                    for part, groups in enumerate(PARTS):
                        if g == groups.start or g == 0 and isinstance(t, int) and t == 0:
                            pe.wait_ge(kb_loaded[part], 16 * (KB_DMAS * (batches(t) - 1) + KB_FIRST[part]))
                wait(pe, bound_read, RT * (G * t + g) + rt - 1)
                bank, rows = a_bank[rt % 2], slice(rt * P, (rt + 1) * P)
                bank_ip = bank[:, :].rearrange("p (j n) -> p j n", j=J)[:, :, TEXT:]
                kb_ip = kb[:, g, :].rearrange("p (j n) -> p j n", j=J)[:, :, TEXT:]
                nc.tensor.matmul(bank[:, :], q_hi[:, g % 2, rows], kb[:, g, :], start=True, stop=False)
                nc.tensor.matmul(bank_ip, q_hi[:, g % 2, rows], kb_lo[:, g, :], start=False, stop=False)
                nc.tensor.matmul(bank_ip, q_lo[:, g % 2, rows], kb_ip,
                                 start=False, stop=True).then_inc(bound_mm, 1)

            def score(t, g, pair):
                if pair == 0:
                    pe.wait_ge(q_stacked[g], 3 * 16 * (t + 1))
                    pe.wait_ge(m_stacked[g], 16 * (t + 1))
                    for part, groups in enumerate(PARTS):
                        if g == groups.start or g == 0 and isinstance(t, int) and t == 0:
                            pe.wait_ge(kst_loaded[part], 16 * (KST_DMAS[part] * (batches(t) - 1) + KST_FIRST[part]))
                wait(pe, exp_done, 2 * (G * t + g) + pair)
                for i in range(2):
                    j = 2 * pair + i
                    last = nc.tensor.matmul(s_bank[0:TEXT, i, :], kst[:, j, g, :], stack[0:STACK, g, j, :],
                                            start=True, stop=True)
                last.then_inc(score_mm, 1)

            def values(t, g):
                u = G * t + g
                if g == 0:
                    pe.wait_ge(v_loaded, 16 * V_DMAS * batches(t))
                pe.wait_ge(exp_done, 2 * u + 2)
                wait(pe, scaled_done, u)
                wait(pe, att_done, u)
                for j in range(J):
                    h = J * g + j
                    nc.tensor.matmul(pv_bank[j * DH:(j + 1) * DH, :], v_sb[:, h * DH:(h + 1) * DH],
                                     probs[:, j, :], start=True, stop=True)
                for j in range(J):
                    last = nc.tensor.matmul(l_bank[j * DH:(j + 1) * DH, :], ones[:, :], probs[:, j, :],
                                            start=True, stop=True)
                last.then_inc(pv_mm, 1)

            def ip_values(t, g):
                pe.wait_ge(sums_read, G * t + g + 1)
                pe.wait_ge(rows_copied, G * t + g + 3)
                if g == 0:
                    pe.wait_ge(vst_loaded, 16 * VST_DMAS * batches(t))
                nc.tensor.matmul(l_bank[:, :], vst[:, g, :], by_row[0:IPROWS, :], start=True, stop=True
                                 ).then_inc(ipv_mm, 1)

            def turn(t, g):
                u = G * t + g
                if runs(*earlier(t, g, 1)):
                    pe.wait_ge(bound_read, RT * u)
                if runs(*earlier(t, g, 3)):
                    pe.wait_ge(ip_p_done, u - 2)
                else:
                    pe.wait_ge(cleared, CLEARED)
                wait(pe, rows_copied, u - 1)
                if g == 3:
                    wait(pe, out_done, G * t)
                for rt in range(RT):
                    last = nc.tensor.transpose(t_bank[0:TURNED, rt * P:(rt + 1) * P], by_query[:, rt, :],
                                               idn[:, :])
                last.then_inc(turned, 1)

            def output(t):
                for m in range(G):
                    bank = q_bank if m % 2 else t_bank
                    if m == 0:
                        pe.wait_ge(rows_copied, G * (t + 1) + 2)
                    elif m == 1:
                        wait(pe, q_lo_done, no_more(G * (t + 1) + 4))
                    else:
                        pe.wait_ge(out_done, G * t + m - 1)
                    cols = slice(m * P, (m + 1) * P)
                    for k in range(G):
                        if m == 0:
                            pe.wait_ge(att_hi_done, G * t + k + 1)
                            pe.wait_ge(att_lo_done, G * t + k + 1)
                        nc.tensor.matmul(bank[:, :], wo_hi[:, k, cols], att_lo[:, k, :], start=k == 0, stop=False)
                        nc.tensor.matmul(bank[:, :], wo_lo[:, k, cols], att_hi[:, k, :], start=False, stop=False)
                        last = nc.tensor.matmul(bank[:, :], wo_hi[:, k, cols], att_hi[:, k, :],
                                                start=False, stop=k == G - 1)
                    last.then_inc(out_mm, 1)

            def last_output(m, k):
                t = TILES - 1
                bank = last_bank(m)
                if k == 0:
                    if m == 0:
                        pe.wait_ge(q_lo_done, UNITS)
                    elif m in (1, 2):
                        pe.wait_ge(bound_read, RT * UNITS)
                    elif m == 3:
                        pe.wait_ge(rows_copied, UNITS + 2)
                    else:
                        pe.wait_ge(exp_done, 2 * UNITS)
                if m == 0:
                    pe.wait_ge(att_hi_done, G * t + k + 1)
                    pe.wait_ge(att_lo_done, G * t + k + 1)
                cols = slice(m * P, (m + 1) * P)
                nc.tensor.matmul(bank, wo_hi[:, k, cols], att_lo[:, k, :], start=k == 0, stop=False)
                nc.tensor.matmul(bank, wo_lo[:, k, cols], att_hi[:, k, :], start=False, stop=False)
                last = nc.tensor.matmul(bank, wo_hi[:, k, cols], att_hi[:, k, :], start=False, stop=k == G - 1)
                if k == G - 1:
                    last.then_inc(out_mm, 1)

            def last_iteration():
                t = TILES
                for g in range(3):
                    a, s, c = earlier(t, g, 1), earlier(t, g, 3), earlier(t, g, 4)
                    score(*s, 0)
                    if g == 0:
                        bound(*a, 0)
                        bound(*a, 1)
                    for m, k in {0: [(0, 0)], 1: [(0, 1), (1, 0)], 2: [(0, 2), (2, 1)]}[g]:
                        last_output(m, k)
                    score(*s, 1)
                    ip_values(*c)
                    if g == 0:
                        bound(*a, 2)
                        bound(*a, 3)
                    for m, k in {0: [], 1: [(1, 1), (2, 0)], 2: [(1, 2), (2, 2)]}[g]:
                        last_output(m, k)
                    values(*s)
                    turn(t, g)
                for m in range(3):
                    last_output(m, 3)
                ip_values(TILES - 1, G - 1)
                for m in (3, 4):
                    for k in range(G - 1):
                        last_output(m, k)
                for m in range(G):
                    last_output(m, G - 1)

            def iteration(t):
                for g in range(G):
                    now, a, s, c = (t, g), earlier(t, g, 1), earlier(t, g, 3), earlier(t, g, 4)
                    if runs(*s):
                        score(*s, 0)
                    if runs(*now):
                        project(*now, 0)
                        project(*now, 1)
                    if runs(*a):
                        bound(*a, 0)
                        bound(*a, 1)
                    if runs(*now):
                        project(*now, 2)
                    if runs(*s):
                        score(*s, 1)
                    if runs(*now):
                        project(*now, 3)
                    if runs(*c):
                        ip_values(*c)
                    if runs(*a):
                        bound(*a, 2)
                    if runs(*a) and not runs(*s):
                        bound(*a, 3)
                    if runs(*now):
                        project(*now, 4)
                    if runs(*a) and runs(*s):
                        bound(*a, 3)
                    if g == 3 and runs(t - 1, 0):
                        output(t - 1)
                    if runs(*s):
                        values(*s)
                    if runs(*a) or runs(*s):
                        turn(t, g)

            iteration(0)
            with pe.Fori(1, TILES) as t:
                iteration(t)
            last_iteration()

        @block.scalar
        def _(act):
            def exps(t, g, pair):
                u = G * t + g
                act.wait_ge(score_mm, 2 * u + pair + 1)
                wait(act, pv_mm, u)
                nc.scalar.activation(probs[:, 2 * pair:2 * pair + 2, :], s_bank[0:TEXT, :, :], ACT.Exp,
                                     scale=SCALE).then_inc(exp_done, 1)

            def copy_rows(t, g):
                u = G * t + g
                act.wait_ge(turned, u)
                wait(act, ipv_mm, u - 3)
                tp, gp = earlier(t, g, 2)
                if runs(tp, gp):
                    act.wait_ge(m_stacked[gp], 16 * (tp + 1))
                nc.scalar.activation(by_row[:, :], t_bank[0:TURNED, :], ACT.Copy).then_inc(rows_copied, 1)

            def att_high(t, g):
                act.wait_ge(att_done, G * t + g + 1)
                wait(act, out_mm, G * t)
                nc.scalar.activation(att_hi[:, g, :], att[:, :], ACT.Copy).then_inc(att_hi_done, 1)

            def q_high(t, g):
                u = G * t + g
                act.wait_ge(q_mm, u + 1)
                lag = 1 if g == 0 else 2
                wait(act, bound_mm, RT * (u - lag + 1))
                tp, gp = earlier(t, g, lag)
                if runs(tp, gp):
                    act.wait_ge(q_stacked[gp], 3 * 16 * (tp + 1))
                nc.scalar.activation(q_hi[:, g % 2, :], project_bank(t, g)[:, :], ACT.Copy).then_inc(q_hi_done, 1)

            def rough_reciprocal(t, g):
                u = G * t + g
                act.wait_ge(pv_mm, u + 1)
                wait(act, refined, u)
                nc.scalar.activation(rough[:, :], l_bank[:, :], ACT.Ln).then_inc(ln_done, 1)
                act.wait_ge(ln_done, u + 1)
                nc.scalar.activation(rough[:, :], rough[:, :], ACT.Exp, scale=-1.0).then_inc(rough_done, 1)

            def ip_exps(t, g):
                u = G * t + g
                act.wait_ge(ip_sub_done, u + 1)
                wait(act, ip_norm_done, u)
                nc.scalar.activation(ip_e[:, :, :], ip_x[:, :, :], ACT.Exp).then_inc(ip_exp_done, 1)

            def x_high(t, k):
                slot = snap(act, x_slot(t, k))
                act.wait_ge(x_loaded[k], 16 * (t + 1))
                if k < G - 1:
                    wait(act, x_used, (G - 1) * (t - 1) + k + 1)
                else:
                    wait(act, q_mm, G * t)
                nc.scalar.activation(x_hi[:, k, :], x_sb[:, bass.ds(slot, W)], ACT.Copy).then_inc(x_hi_done, 1)

            def iteration(t):
                for g in range(G):
                    now, a, s, c = (t, g), earlier(t, g, 1), earlier(t, g, 3), earlier(t, g, 4)
                    split = g == G - 1 and has_next(t)
                    if runs(*s):
                        exps(*s, 0)
                    if split:
                        x_high(t + 1, 0)
                    if runs(*s):
                        exps(*s, 1)
                    if split:
                        x_high(t + 1, 1)
                    if runs(*c):
                        att_high(*c)
                    if split:
                        x_high(t + 1, 2)
                        x_high(t + 1, 3)
                    if runs(*now):
                        q_high(*now)
                    if split:
                        x_high(t + 1, 4)
                    if runs(*s):
                        rough_reciprocal(*s)
                    if runs(*a) or runs(*s):
                        copy_rows(t, g)
                    if runs(*a):
                        ip_exps(*a)

            for k in range(G):
                x_high(0, k)
            iteration(0)
            with act.Fori(1, TILES - 1) as t:
                iteration(t)
            iteration(TILES - 1)
            iteration(TILES)

        @block.vector
        def _(dve):
            def read_bound(t, g, rt):
                u = G * t + g
                scores = a_bank[rt % 2][:, :].rearrange("p (j n) -> p j n", j=J)
                dve.wait_ge(bound_mm, RT * u + rt + 1)
                if rt == 0:
                    wait(dve, turned, u)
                    wait(dve, ip_sub_done, u)
                nc.vector.tensor_reduce(by_query[:, rt, IPROWS:TURNED],
                                        scores[:, :, 0:TEXT], AX_X, ALU.max,
                                        negate=True)
                row = mask[:, bass.ds(t * RT + rt, 1), :].to_broadcast([P, J, IP])
                nc.vector.scalar_tensor_tensor(
                    ip_s[:, rt * J:(rt + 1) * J, :],
                    scores[:, :, TEXT:],
                    SCALE, row, ALU.mult, ALU.add).then_inc(bound_read, 1)

            def ip_sums(t, g):
                u = G * t + g
                dve.wait_ge(ip_exp_done, u + 1)
                wait(dve, ip_rec_done, u)
                nc.vector.tensor_reduce(ip_sum[:, :], ip_e[:, :, :], AX_X, ALU.add).then_inc(ip_sum_done, 1)
                wait(dve, ip_norm_done, u)
                dve.wait_ge(ip_sum_done, u + 1)
                nc.vector.reciprocal(ip_rec[:, :], ip_sum[:, :]).then_inc(ip_rec_done, 1)

            def scale_values(t, g):
                u = G * t + g
                dve.wait_ge(rough_done, u + 1)
                wait(dve, att_lo_done, u)
                nc.vector.tensor_tensor(att[:, :], l_bank[:, :], rough[:, :], ALU.mult).then_inc(sums_read, 1)
                dve.wait_ge(sums_read, u + 1)
                nc.vector.scalar_tensor_tensor(att[:, :], att[:, :], 2.0, rough[:, :], ALU.subtract, ALU.mult,
                                               reverse0=True).then_inc(refined, 1)
                dve.wait_ge(refined, u + 1)
                nc.vector.tensor_tensor(att[:, :], pv_bank[:, :], att[:, :], ALU.mult).then_inc(scaled_done, 1)

            def add_ip(t, g):
                u = G * t + g
                dve.wait_ge(ipv_mm, u + 1)
                dve.wait_ge(scaled_done, u + 1)
                nc.vector.tensor_tensor(att[:, :], l_bank[:, :], att[:, :], ALU.add).then_inc(att_done, 1)

            def ip_shift(t, g):
                u = G * t + g
                dve.wait_ge(bound_read, RT * (u + 1))
                nc.vector.tensor_reduce(ip_max[:, :], ip_s[:, :, :], AX_X, ALU.max).then_inc(ip_max_done, 1)
                wait(dve, ip_exp_done, u)
                dve.wait_ge(ip_max_done, u + 1)
                nc.vector.tensor_tensor(ip_x[:, :, :], ip_s[:, :, :],
                                        ip_max[:, :].unsqueeze(2).to_broadcast([P, RT * J, IP]),
                                        ALU.subtract).then_inc(ip_sub_done, 1)

            def q_low(t, g):
                u = G * t + g
                dve.wait_ge(q_hi_done, u + 1)
                nc.vector.tensor_tensor(q_lo[:, g % 2, :], project_bank(t, g)[:, :],
                                        q_hi[:, g % 2, :].bitcast(F32), ALU.subtract).then_inc(q_lo_done, 1)

            def finish(t):
                for m in range(G):
                    residual = x_sb[:, bass.ds(snap(dve, x_slot(t, m)), W)]
                    wait(dve, out_stored[m % 2], 16 * stores_before(t, m))
                    dve.wait_ge(out_mm, G * t + m + 1)
                    last_tile = isinstance(t, int) and t == TILES - 1
                    bank = last_bank(m) if last_tile else (q_bank if m % 2 else t_bank)[:, :]
                    nc.vector.scalar_tensor_tensor(out_sb[:, m % 2, :], bank, bias[:, m:m + 1], residual,
                                                   ALU.add, ALU.add).then_inc(out_done, 1)

            def iteration(t):
                for g in range(G):
                    now, a, i, c = (t, g), earlier(t, g, 1), earlier(t, g, 2), earlier(t, g, 4)
                    if runs(*c):
                        scale_values(*c)
                    if runs(*a):
                        read_bound(*a, 0)
                        read_bound(*a, 1)
                    if runs(*i):
                        ip_sums(*i)
                    if runs(*c):
                        add_ip(*c)
                    if runs(*a):
                        read_bound(*a, 2)
                        read_bound(*a, 3)
                        ip_shift(*a)
                    if runs(*now):
                        q_low(*now)
                    if g == 0 and isinstance(t, int) and t == 0:
                        nc.vector.memset(kst[3 * DH:STACK, :, :, :].bitcast(F32), 1.0).then_inc(cleared, 1)
                    if g == 3 and runs(t - 1, 0):
                        finish(t - 1)

            for k in range(G):
                dve.wait_ge(x_hi_done, k + 1)
                nc.vector.tensor_tensor(x_lo[:, k, :], x_sb[:, k * W:(k + 1) * W], x_hi[:, k, :].bitcast(F32),
                                        ALU.subtract).then_inc(x_lo_done, 1)
            nc.vector.memset(ones[:, :], 1.0).then_inc(cleared, 1)
            nc.vector.memset(by_query[:, :, :], 0.0).then_inc(cleared, 1)
            over_tiles(dve, iteration)

        @block.gpsimd
        def _(pool):
            def ip_norm(t, g):
                u = G * t + g
                pool.wait_ge(ip_rec_done, u + 1)
                wait(pool, ip_p_done, u)
                nc.gpsimd.tensor_tensor(ip_n[:, :, :].rearrange("p r (j n) -> p (r j) n", j=J), ip_e[:, :, :],
                                        ip_rec[:, :].unsqueeze(2).to_broadcast([P, RT * J, IP]),
                                        ALU.mult).then_inc(ip_norm_done, 1)

            def ip_split(t, g):
                u = G * t + g
                pool.wait_ge(ip_norm_done, u + 1)
                pool.wait_ge(turned, u + 2)
                hi, lo, again = (by_query[:, :, i * J * IP:(i + 1) * J * IP] for i in range(3))
                unit = one[:, :].unsqueeze(2).to_broadcast([P, RT, J * IP])
                nc.gpsimd.tensor_tensor(hi.bitcast(F32R), ip_n[:, :, :], unit, ALU.mult).then_inc(ip_hi_done, 1)
                nc.gpsimd.tensor_tensor(again.bitcast(F32R), ip_n[:, :, :], unit, ALU.mult).then_inc(ip_hi_done, 1)
                pool.wait_ge(ip_hi_done, 2 * (u + 1))
                nc.gpsimd.tensor_tensor(lo.bitcast(F32R), ip_n[:, :, :], hi, ALU.subtract).then_inc(ip_p_done, 1)

            def att_low(t, g):
                pool.wait_ge(att_hi_done, G * t + g + 1)
                nc.gpsimd.tensor_tensor(att_lo[:, g, :], att[:, :], att_hi[:, g, :].bitcast(F32),
                                        ALU.subtract).then_inc(att_lo_done, 1)

            def x_low(t, k):
                place = x_sb[:, bass.ds(snap(pool, x_slot(t, k)), W)]
                pool.wait_ge(x_hi_done, G * t + k + 1)
                nc.gpsimd.tensor_tensor(x_lo[:, k, :], place, x_hi[:, k, :].bitcast(F32),
                                        ALU.subtract).then_inc(x_lo_done, 1)

            def iteration(t):
                for g in range(G):
                    i, s, c = earlier(t, g, 2), earlier(t, g, 3), earlier(t, g, 4)
                    split = g == G - 1 and has_next(t)
                    if runs(*s):
                        ip_split(*s)
                    if split:
                        x_low(t + 1, 0)
                    if runs(*i):
                        ip_norm(*i)
                    if split:
                        x_low(t + 1, 1)
                    if runs(*c):
                        att_low(*c)
                    if split:
                        for k in range(2, G):
                            x_low(t + 1, k)

            nc.gpsimd.memset(vst[:, :, :].bitcast(F32), 0.0).then_inc(cleared, 1)
            nc.gpsimd.memset(one[:, :], 1.0).then_inc(cleared, 1)
            pool.wait_ge(cleared, CLEARED)
            iteration(0)
            with pool.Fori(1, TILES - 1) as t:
                iteration(t)
            iteration(TILES - 1)
            iteration(TILES)


def kernel(**inputs):
    import concourse.bacc as bacc
    from concourse.bass_utils import run_bass_kernel_spmd

    def a(name):
        return np.asarray(inputs[name])

    def by_feature(w):
        return np.ascontiguousarray(w.reshape(w.shape[0], G, J, DH).transpose(0, 1, 3, 2).reshape(w.shape[0], D))

    xs = np.linspace(0.0, 1.0, GRID_W, dtype=np.float32)
    ys = np.linspace(0.0, 1.0, GRID_H, dtype=np.float32)
    token = np.arange(S).reshape(S // P, P)
    gx = xs[token[0] % GRID_W].reshape(P, 1)
    gy = ys[token // GRID_W].T

    c = a("ctx_2048")
    arrays = {
        "xT": np.ascontiguousarray(a("x").reshape(B * S, D).T),
        "ctxT": np.ascontiguousarray(np.concatenate([c[:, :TEXT].reshape(B * TEXT, C), c[:, TEXT:].reshape(B * IP, C)]).T),
        "boxes": a("fside_Bx4x4_0").reshape(1, B * BOXES * 4),
        "gx": gx, "gy": np.ascontiguousarray(gy),
        "ident": np.eye(P, dtype=np.float32),
        "wq": by_feature(a("L0_xattn_w_q")),
        "wk": by_feature(a("L0_xattn_w_k")),
        "wv": a("L0_xattn_w_v"),
        "wkip": by_feature(a("L0_xattn_w_k_ip")),
        "wvip": a("L0_xattn_w_v_ip"),
        "wo": a("L0_xattn_w_out"),
        "bo": np.ascontiguousarray(a("L0_xattn_b_out").reshape(G, P).T.reshape(D)),
    }
    nc = bacc.Bacc("TRN2", target_bir_lowering=False, num_devices=1)
    args = [nc.dram_tensor(n, v.shape, mybir.dt.from_np(v.dtype), kind="ExternalInput").ap()
            for n, v in arrays.items()]
    args.append(nc.dram_tensor("outT", (D, B * S), F32, kind="ExternalOutput").ap())
    xattn_kernel(nc, *args)
    r = run_bass_kernel_spmd(nc, [arrays], core_ids=[0])
    return np.ascontiguousarray(r.results[0]["outT"].T).reshape(B, S, D)
```
